# Optimizing a Trainium2 kernel written in Bass

```python
import numpy as np
import jax
import jax.numpy as jnp

def _softmax(x, axis=-1):
    return jax.nn.softmax(x, axis=axis)

def _gelu(x):
    return jax.nn.gelu(x, approximate=True)

def _silu(x):
    return jax.nn.silu(x)

def _sigmoid(x):
    return jax.nn.sigmoid(x)

def _layernorm(x, axis=-1, eps=1e-05):
    m = jnp.mean(x, axis=axis, keepdims=True)
    v = jnp.var(x, axis=axis, keepdims=True)
    return (x - m) / jnp.sqrt(v + eps)

def _scatter_add(tgt, idx, src, axis=0):
    return tgt.at[idx].add(src)

def _segment_sum(src, seg, n):
    return jax.ops.segment_sum(src, seg, n)
kernel_name = 'mk_hybrid_d2_jaxref_r8_fdbd19'

def setup_inputs(seed: int=0):
    np.random.seed(seed)
    _w = jnp.asarray

    def _L0_attn_a_setup():
        import jax, jax.numpy as jnp
        import numpy as np
        from math import sqrt
        D_MODEL = 128
        NUM_HEADS = 16
        MASK_VAL = -100000000.0

        def _proj_heads(x, w, h):
            d = w.shape[0] // h
            w = w.reshape(h, d, w.shape[1])
            return jnp.einsum('bsi,hdi->bhsd', x, w)
        key = jax.random.key(seed)
        k1, k2, k3, k4, k5 = jax.random.split(key, 5)
        scale = 1.0 / sqrt(D_MODEL)
        return {'in_features': jax.random.normal(k1, (2, 256, D_MODEL), dtype=jnp.float32), 'q_proj_weight': jax.random.normal(k2, (D_MODEL, D_MODEL), dtype=jnp.float32) * scale, 'k_proj_weight': jax.random.normal(k3, (D_MODEL, D_MODEL), dtype=jnp.float32) * scale, 'v_proj_weight': jax.random.normal(k4, (D_MODEL, D_MODEL), dtype=jnp.float32) * scale, 'o_proj_weight': jax.random.normal(k5, (D_MODEL, D_MODEL), dtype=jnp.float32) * scale}
    _L0_attn_a_in = _L0_attn_a_setup()

    def _L0_attn_b_setup():
        import jax, jax.numpy as jnp
        import numpy as np
        SCALE = 1.0 / np.sqrt(64.0)
        key = jax.random.key(seed)
        k1, k2 = jax.random.split(key)
        x = jax.random.normal(k1, (8, 256, 128), dtype=jnp.float32)
        kernel = jax.random.normal(k2, (3, 128, 128), dtype=jnp.float32) * 0.02
        return {'x': x, 'kernel': kernel}
    _L0_attn_b_in = _L0_attn_b_setup()

    def _L0_ffn_setup():
        import jax, jax.numpy as jnp
        import numpy as np
        DIM = 128
        DEPTH = 6
        HEADS = 16
        DIM_HEAD = 64
        WINDOW = 32
        INNER = HEADS * DIM_HEAD
        DIM_INNER = int(DIM * 4 * 2 / 3)
        QK_SCALE = 8.0

        def shift_tokens(t):
            a, s = jnp.split(t, 2, -1)
            s = jnp.pad(s, ((0, 0), (1, 0), (0, 0)))[:, :-1]
            return jnp.concatenate([a, s], -1)

        def l2norm(t):
            return t / jnp.maximum(jnp.linalg.norm(t, axis=-1, keepdims=True), 1e-12)

        def rotate_half(x):
            x1, x2 = jnp.split(x, 2, -1)
            return jnp.concatenate([-x2, x1], -1)

        def rotary_tables(n):
            half = jnp.arange(0, DIM_HEAD, 2, dtype=jnp.float32)
            inv_freq = 1.0 / 10000.0 ** (half / DIM_HEAD)
            t = jnp.arange(n, dtype=jnp.float32)
            freqs = t[:, None] * inv_freq[None, :]
            freqs = jnp.concatenate([freqs, freqs], -1)
            base_scale = (half + 0.4 * DIM_HEAD) / (1.4 * DIM_HEAD)
            power = (t - n // 2) / (WINDOW // 2)
            scale = base_scale[None, :] ** power[:, None]
            scale = jnp.concatenate([scale, scale], -1)
            return (freqs, scale)

        def local_attention(q, k, v):
            b, h, n, d = q.shape
            w = WINDOW
            nw = n // w
            bq = q.reshape(b, h, nw, w, d)
            bk = k.reshape(b, h, nw, w, d)
            bv = v.reshape(b, h, nw, w, d)

            def look(t):
                p = jnp.pad(t, ((0, 0), (0, 0), (1, 0), (0, 0), (0, 0)))
                return jnp.concatenate([p[:, :, :nw], p[:, :, 1:]], axis=3)
            bk2, bv2 = (look(bk), look(bv))
            seq = jnp.arange(n).reshape(nw, w)
            seq_p = jnp.pad(seq, ((1, 0), (0, 0)), constant_values=-1)
            jt = jnp.concatenate([seq_p[:nw], seq_p[1:]], axis=1)
            it = seq[:, :, None]
            jb = jt[:, None, :]
            mask = (it < jb) | (it > jb + w) | (jb == -1)
            sim = jnp.einsum('bhwie,bhwje->bhwij', bq, bk2) * QK_SCALE
            sim = jnp.where(mask, -jnp.finfo(sim.dtype).max, sim)
            attn = jax.nn.softmax(sim, -1)
            out = jnp.einsum('bhwij,bhwje->bhwie', attn, bv2)
            return out.reshape(b, h, n, d)

        def attn_layer(x, Wqkv, qs, ksc, Wo):
            b, n, _ = x.shape
            qkv = x @ Wqkv
            q, k, v = jnp.split(qkv, 3, -1)
            sh = lambda t: t.reshape(b, n, HEADS, DIM_HEAD).transpose(0, 2, 1, 3)
            q, k, v = (sh(q), sh(k), sh(v))
            q = l2norm(q) * qs
            k = l2norm(k) * ksc
            freqs, scale = rotary_tables(n)
            cos, sin = (jnp.cos(freqs), jnp.sin(freqs))
            q = q * cos * scale + rotate_half(q) * sin * scale
            inv = 1.0 / scale
            k = k * cos * inv + rotate_half(k) * sin * inv
            out = local_attention(q, k, v)
            out = out.transpose(0, 2, 1, 3).reshape(b, n, INNER)
            return out @ Wo

        def ffn_layer(x, g, bln, W1, b1, W2, b2):
            mu = x.mean(-1, keepdims=True)
            var = ((x - mu) ** 2).mean(-1, keepdims=True)
            xn = (x - mu) / jnp.sqrt(var + 1e-05) * g + bln
            hg = xn @ W1 + b1
            a, gate = jnp.split(hg, 2, -1)
            return a * jax.nn.gelu(gate, approximate=False) @ W2 + b2
        key = jax.random.key(seed)
        ks = jax.random.split(key, 8)
        B, N = (2, 256)
        init = lambda k, shape: jax.random.normal(k, shape, jnp.float32) * 0.02
        return {'x': jax.random.normal(ks[0], (B, N, DIM), jnp.float32), 'Wqkv': init(ks[1], (DEPTH, DIM, 3 * INNER)), 'q_scale': jnp.ones((DEPTH, DIM_HEAD), jnp.float32), 'k_scale': jnp.ones((DEPTH, DIM_HEAD), jnp.float32), 'Wo': init(ks[2], (DEPTH, INNER, DIM)), 'ln_g': jnp.ones((DEPTH, DIM), jnp.float32), 'ln_b': jnp.zeros((DEPTH, DIM), jnp.float32), 'W1': init(ks[3], (DEPTH, DIM, 2 * DIM_INNER)), 'b1': jnp.zeros((DEPTH, 2 * DIM_INNER), jnp.float32), 'W2': init(ks[4], (DEPTH, DIM_INNER, DIM)), 'b2': jnp.zeros((DEPTH, DIM), jnp.float32)}
    _L0_ffn_in = _L0_ffn_setup()

    def _L1_attn_a_setup():
        import jax, jax.numpy as jnp
        import numpy as np
        S, B, E, H = (256, 2, 128, 16)
        HD = E // H
        key = jax.random.key(seed)
        ks = jax.random.split(key, 5)
        return {'query': jax.random.normal(ks[0], (S, B, E), dtype=jnp.float32), 'key': jax.random.normal(ks[1], (S, B, E), dtype=jnp.float32), 'value': jax.random.normal(ks[2], (S, B, E), dtype=jnp.float32), 'in_proj_weight': jax.random.normal(ks[3], (3 * E, E), dtype=jnp.float32) * E ** (-0.5), 'out_weight': jax.random.normal(ks[4], (E, E), dtype=jnp.float32) * E ** (-0.5)}
    _L1_attn_a_in = _L1_attn_a_setup()

    def _L1_attn_b_setup():
        import jax, jax.numpy as jnp
        import numpy as np
        HEADS = 16

        def _binarize(W):
            alpha = jnp.mean(jnp.abs(W), axis=tuple(range(1, W.ndim)), keepdims=True)
            B = W + jax.lax.stop_gradient(jnp.sign(W) - W)
            return alpha * B

        def _binlinear(x, W, b):
            Wb = _binarize(W)
            return jnp.einsum('btc,oc->bto', x, Wb) + b
        key = jax.random.key(seed)
        ks = jax.random.split(key, 9)
        dim = 128
        B, T = (4, 256)
        inp = {'x': jax.random.normal(ks[0], (B, T, dim), jnp.float32), 'Wq': jax.random.normal(ks[1], (dim, dim), jnp.float32) * 0.02, 'bq': jax.random.normal(ks[2], (dim,), jnp.float32) * 0.02, 'Wk': jax.random.normal(ks[3], (dim, dim), jnp.float32) * 0.02, 'bk': jax.random.normal(ks[4], (dim,), jnp.float32) * 0.02, 'Wv': jax.random.normal(ks[5], (dim, dim), jnp.float32) * 0.02, 'bv': jax.random.normal(ks[6], (dim,), jnp.float32) * 0.02, 'Wp': jax.random.normal(ks[7], (dim, dim), jnp.float32) * 0.02, 'bp': jax.random.normal(ks[8], (dim,), jnp.float32) * 0.02}
        return inp
    _L1_attn_b_in = _L1_attn_b_setup()

    def _L1_ffn_setup():
        import jax, jax.numpy as jnp
        import numpy as np
        E = 8
        D = 128
        F = 512
        S, B = (256, 2)
        LN_EPS = 1e-05

        def _moe_forward(input_features, centroids, ln_g, ln_b, W1, b1, W2, b2):
            s, b, d = input_features.shape
            x = jnp.swapaxes(input_features, 0, 1).reshape(-1, d)
            logits = x.astype(jnp.float32) @ centroids.astype(jnp.float32).T
            assign = jnp.argmax(logits, axis=-1)
            onehot = jax.nn.one_hot(assign, E, dtype=x.dtype)
            disp = jnp.einsum('te,td->etd', onehot, x)
            mu = disp.mean(-1, keepdims=True)
            var = disp.var(-1, keepdims=True)
            xn = (disp - mu) * jax.lax.rsqrt(var + LN_EPS)
            xn = xn * ln_g[:, None, :] + ln_b[:, None, :]
            h = jax.nn.relu(jnp.einsum('etd,edf->etf', xn, W1) + b1[:, None, :])
            y = jnp.einsum('etf,efd->etd', h, W2) + b2[:, None, :]
            y = disp + y
            out = jnp.einsum('te,etd->td', onehot, y)
            return jnp.swapaxes(out.reshape(b, s, d), 0, 1)
        key = jax.random.key(seed)
        ks = jax.random.split(key, 8)
        scale_in = 1.0 / np.sqrt(D)
        scale_ff = 1.0 / np.sqrt(F)
        return {'input_features': jax.random.normal(ks[0], (S, B, D), dtype=jnp.float32), 'centroids': jax.random.normal(ks[1], (E, D), dtype=jnp.float32) * scale_in, 'ln_g': jnp.ones((E, D), dtype=jnp.float32), 'ln_b': jnp.zeros((E, D), dtype=jnp.float32), 'W1': jax.random.normal(ks[2], (E, D, F), dtype=jnp.float32) * scale_in, 'b1': jax.random.normal(ks[3], (E, F), dtype=jnp.float32) * 0.01, 'W2': jax.random.normal(ks[4], (E, F, D), dtype=jnp.float32) * scale_ff, 'b2': jax.random.normal(ks[5], (E, D), dtype=jnp.float32) * 0.01}
    _L1_ffn_in = _L1_ffn_setup()
    _d = {'L0_attn_a_in_features': _L0_attn_a_in['in_features'], 'L0_attn_a_q_proj_weight': _L0_attn_a_in['q_proj_weight'], 'L0_attn_a_k_proj_weight': _L0_attn_a_in['k_proj_weight'], 'L0_attn_a_v_proj_weight': _L0_attn_a_in['v_proj_weight'], 'L0_attn_a_o_proj_weight': _L0_attn_a_in['o_proj_weight'], 'L0_attn_b_kernel': _L0_attn_b_in['kernel'], 'L0_ffn_Wqkv': _L0_ffn_in['Wqkv'], 'L0_ffn_q_scale': _L0_ffn_in['q_scale'], 'L0_ffn_k_scale': _L0_ffn_in['k_scale'], 'L0_ffn_Wo': _L0_ffn_in['Wo'], 'L0_ffn_ln_g': _L0_ffn_in['ln_g'], 'L0_ffn_ln_b': _L0_ffn_in['ln_b'], 'L0_ffn_W1': _L0_ffn_in['W1'], 'L0_ffn_b1': _L0_ffn_in['b1'], 'L0_ffn_W2': _L0_ffn_in['W2'], 'L0_ffn_b2': _L0_ffn_in['b2'], 'L1_attn_a_key': _L1_attn_a_in['key'], 'L1_attn_a_value': _L1_attn_a_in['value'], 'L1_attn_a_in_proj_weight': _L1_attn_a_in['in_proj_weight'], 'L1_attn_a_out_weight': _L1_attn_a_in['out_weight'], 'L1_attn_b_Wq': _L1_attn_b_in['Wq'], 'L1_attn_b_bq': _L1_attn_b_in['bq'], 'L1_attn_b_Wk': _L1_attn_b_in['Wk'], 'L1_attn_b_bk': _L1_attn_b_in['bk'], 'L1_attn_b_Wv': _L1_attn_b_in['Wv'], 'L1_attn_b_bv': _L1_attn_b_in['bv'], 'L1_attn_b_Wp': _L1_attn_b_in['Wp'], 'L1_attn_b_bp': _L1_attn_b_in['bp'], 'L1_ffn_centroids': _L1_ffn_in['centroids'], 'L1_ffn_ln_g': _L1_ffn_in['ln_g'], 'L1_ffn_ln_b': _L1_ffn_in['ln_b'], 'L1_ffn_W1': _L1_ffn_in['W1'], 'L1_ffn_b1': _L1_ffn_in['b1'], 'L1_ffn_W2': _L1_ffn_in['W2'], 'L1_ffn_b2': _L1_ffn_in['b2']}
    _x0 = _d['L0_attn_a_in_features']
    _d['L0_attn_a_in_features'] = jax.random.normal(jax.random.fold_in(jax.random.key(seed), 1), (8, 256, 128), dtype=_x0.dtype)
    del _x0
    return _d

def reference(L0_attn_a_in_features, L0_attn_a_q_proj_weight, L0_attn_a_k_proj_weight, L0_attn_a_v_proj_weight, L0_attn_a_o_proj_weight, L0_attn_b_kernel, L0_ffn_Wqkv, L0_ffn_q_scale, L0_ffn_k_scale, L0_ffn_Wo, L0_ffn_ln_g, L0_ffn_ln_b, L0_ffn_W1, L0_ffn_b1, L0_ffn_W2, L0_ffn_b2, L1_attn_a_key, L1_attn_a_value, L1_attn_a_in_proj_weight, L1_attn_a_out_weight, L1_attn_b_Wq, L1_attn_b_bq, L1_attn_b_Wk, L1_attn_b_bk, L1_attn_b_Wv, L1_attn_b_bv, L1_attn_b_Wp, L1_attn_b_bp, L1_ffn_centroids, L1_ffn_ln_g, L1_ffn_ln_b, L1_ffn_W1, L1_ffn_b1, L1_ffn_W2, L1_ffn_b2):

    def _L0_attn_a_ref(in_features, q_proj_weight, k_proj_weight, v_proj_weight, o_proj_weight):
        import jax, jax.numpy as jnp
        import numpy as np
        from math import sqrt
        D_MODEL = 128
        NUM_HEADS = 16
        MASK_VAL = -100000000.0

        def _proj_heads(x, w, h):
            d = w.shape[0] // h
            w = w.reshape(h, d, w.shape[1])
            return jnp.einsum('bsi,hdi->bhsd', x, w)
        h = NUM_HEADS
        b, s, _ = in_features.shape
        q = _proj_heads(in_features, q_proj_weight, h)
        k = _proj_heads(in_features, k_proj_weight, h)
        v = _proj_heads(in_features, v_proj_weight, h)
        d_k = q.shape[-1]
        mask = jnp.triu(jnp.full((s, s), MASK_VAL, dtype=q.dtype), k=1)[None, None]
        scores = jnp.einsum('bhqd,bhkd->bhqk', q, k) / sqrt(d_k) + mask
        attn = jax.nn.softmax(scores, axis=-1)
        out = jnp.einsum('bhqk,bhkd->bhqd', attn, v)
        out = out.transpose(0, 2, 1, 3).reshape(b, s, -1)
        return jnp.einsum('bsv,mv->bsm', out, o_proj_weight)

    def _L0_attn_b_ref(x, kernel):
        import jax, jax.numpy as jnp
        import numpy as np
        SCALE = 1.0 / np.sqrt(64.0)
        wq = jnp.einsum('bsd,de->bse', x, kernel[0])
        wk = jnp.einsum('bsd,de->bse', x, kernel[1])
        wv = jnp.einsum('bsd,de->bse', x, kernel[2])
        scores = jnp.einsum('bqe,bke->bqk', wq, wk) * SCALE
        attn = jax.nn.softmax(scores, axis=-1)
        return jnp.einsum('bqk,bke->bqe', attn, wv)

    def _L0_ffn_ref(x, Wqkv, q_scale, k_scale, Wo, ln_g, ln_b, W1, b1, W2, b2):
        import jax, jax.numpy as jnp
        import numpy as np
        DIM = 128
        DEPTH = 6
        HEADS = 16
        DIM_HEAD = 64
        WINDOW = 32
        INNER = HEADS * DIM_HEAD
        DIM_INNER = int(DIM * 4 * 2 / 3)
        QK_SCALE = 8.0

        def shift_tokens(t):
            a, s = jnp.split(t, 2, -1)
            s = jnp.pad(s, ((0, 0), (1, 0), (0, 0)))[:, :-1]
            return jnp.concatenate([a, s], -1)

        def l2norm(t):
            return t / jnp.maximum(jnp.linalg.norm(t, axis=-1, keepdims=True), 1e-12)

        def rotate_half(x):
            x1, x2 = jnp.split(x, 2, -1)
            return jnp.concatenate([-x2, x1], -1)

        def rotary_tables(n):
            half = jnp.arange(0, DIM_HEAD, 2, dtype=jnp.float32)
            inv_freq = 1.0 / 10000.0 ** (half / DIM_HEAD)
            t = jnp.arange(n, dtype=jnp.float32)
            freqs = t[:, None] * inv_freq[None, :]
            freqs = jnp.concatenate([freqs, freqs], -1)
            base_scale = (half + 0.4 * DIM_HEAD) / (1.4 * DIM_HEAD)
            power = (t - n // 2) / (WINDOW // 2)
            scale = base_scale[None, :] ** power[:, None]
            scale = jnp.concatenate([scale, scale], -1)
            return (freqs, scale)

        def local_attention(q, k, v):
            b, h, n, d = q.shape
            w = WINDOW
            nw = n // w
            bq = q.reshape(b, h, nw, w, d)
            bk = k.reshape(b, h, nw, w, d)
            bv = v.reshape(b, h, nw, w, d)

            def look(t):
                p = jnp.pad(t, ((0, 0), (0, 0), (1, 0), (0, 0), (0, 0)))
                return jnp.concatenate([p[:, :, :nw], p[:, :, 1:]], axis=3)
            bk2, bv2 = (look(bk), look(bv))
            seq = jnp.arange(n).reshape(nw, w)
            seq_p = jnp.pad(seq, ((1, 0), (0, 0)), constant_values=-1)
            jt = jnp.concatenate([seq_p[:nw], seq_p[1:]], axis=1)
            it = seq[:, :, None]
            jb = jt[:, None, :]
            mask = (it < jb) | (it > jb + w) | (jb == -1)
            sim = jnp.einsum('bhwie,bhwje->bhwij', bq, bk2) * QK_SCALE
            sim = jnp.where(mask, -jnp.finfo(sim.dtype).max, sim)
            attn = jax.nn.softmax(sim, -1)
            out = jnp.einsum('bhwij,bhwje->bhwie', attn, bv2)
            return out.reshape(b, h, n, d)

        def attn_layer(x, Wqkv, qs, ksc, Wo):
            b, n, _ = x.shape
            qkv = x @ Wqkv
            q, k, v = jnp.split(qkv, 3, -1)
            sh = lambda t: t.reshape(b, n, HEADS, DIM_HEAD).transpose(0, 2, 1, 3)
            q, k, v = (sh(q), sh(k), sh(v))
            q = l2norm(q) * qs
            k = l2norm(k) * ksc
            freqs, scale = rotary_tables(n)
            cos, sin = (jnp.cos(freqs), jnp.sin(freqs))
            q = q * cos * scale + rotate_half(q) * sin * scale
            inv = 1.0 / scale
            k = k * cos * inv + rotate_half(k) * sin * inv
            out = local_attention(q, k, v)
            out = out.transpose(0, 2, 1, 3).reshape(b, n, INNER)
            return out @ Wo

        def ffn_layer(x, g, bln, W1, b1, W2, b2):
            mu = x.mean(-1, keepdims=True)
            var = ((x - mu) ** 2).mean(-1, keepdims=True)
            xn = (x - mu) / jnp.sqrt(var + 1e-05) * g + bln
            hg = xn @ W1 + b1
            a, gate = jnp.split(hg, 2, -1)
            return a * jax.nn.gelu(gate, approximate=False) @ W2 + b2
        for i in range(DEPTH):
            x = attn_layer(shift_tokens(x), Wqkv[i], q_scale[i], k_scale[i], Wo[i]) + x
            x = ffn_layer(shift_tokens(x), ln_g[i], ln_b[i], W1[i], b1[i], W2[i], b2[i]) + x
        return x

    def _L1_attn_a_ref(query, key, value, in_proj_weight, out_weight):
        import jax, jax.numpy as jnp
        import numpy as np
        S, B, E, H = (256, 2, 128, 16)
        HD = E // H
        seq_len, bsz, embed_dim = query.shape
        head_dim = embed_dim // H
        scaling = head_dim ** (-0.5)
        qkv = jnp.einsum('sbe,fe->sbf', query, in_proj_weight)
        qkv = qkv.reshape(seq_len, bsz, H, 3, head_dim)
        q = qkv[..., 0, :]
        k = qkv[..., 1, :]
        v = qkv[..., 2, :]
        scores = jnp.einsum('sbhd,tbhd->bhst', q, k) * scaling
        probs = jax.nn.softmax(scores, axis=-1)
        attn = jnp.einsum('bhst,tbhd->sbhd', probs, v)
        attn = attn.reshape(seq_len, bsz, embed_dim)
        out = jnp.einsum('sbe,fe->sbf', attn, out_weight)
        return out

    def _L1_attn_b_ref(x, Wq, bq, Wk, bk, Wv, bv, Wp, bp):
        import jax, jax.numpy as jnp
        import numpy as np
        HEADS = 16

        def _binarize(W):
            alpha = jnp.mean(jnp.abs(W), axis=tuple(range(1, W.ndim)), keepdims=True)
            B = W + jax.lax.stop_gradient(jnp.sign(W) - W)
            return alpha * B

        def _binlinear(x, W, b):
            Wb = _binarize(W)
            return jnp.einsum('btc,oc->bto', x, Wb) + b
        B, T, C = x.shape
        H = HEADS
        Dh = C // H
        scale = Dh ** (-0.5)

        def split_heads(t):
            return t.reshape(B, T, H, Dh).transpose(0, 2, 1, 3)
        q = split_heads(_binlinear(x, Wq, bq))
        k = split_heads(_binlinear(x, Wk, bk))
        v = split_heads(_binlinear(x, Wv, bv))
        att = jnp.einsum('bhtd,bhsd->bhts', q, k) * scale
        att = jax.nn.softmax(att, axis=-1)
        y = jnp.einsum('bhts,bhsd->bhtd', att, v)
        y = y.transpose(0, 2, 1, 3).reshape(B, T, C)
        return _binlinear(y, Wp, bp)

    def _L1_ffn_ref(input_features, centroids, ln_g, ln_b, W1, b1, W2, b2):
        import jax, jax.numpy as jnp
        import numpy as np
        E = 8
        D = 128
        F = 512
        S, B = (256, 2)
        LN_EPS = 1e-05

        def _moe_forward(input_features, centroids, ln_g, ln_b, W1, b1, W2, b2):
            s, b, d = input_features.shape
            x = jnp.swapaxes(input_features, 0, 1).reshape(-1, d)
            logits = x.astype(jnp.float32) @ centroids.astype(jnp.float32).T
            assign = jnp.argmax(logits, axis=-1)
            onehot = jax.nn.one_hot(assign, E, dtype=x.dtype)
            disp = jnp.einsum('te,td->etd', onehot, x)
            mu = disp.mean(-1, keepdims=True)
            var = disp.var(-1, keepdims=True)
            xn = (disp - mu) * jax.lax.rsqrt(var + LN_EPS)
            xn = xn * ln_g[:, None, :] + ln_b[:, None, :]
            h = jax.nn.relu(jnp.einsum('etd,edf->etf', xn, W1) + b1[:, None, :])
            y = jnp.einsum('etf,efd->etd', h, W2) + b2[:, None, :]
            y = disp + y
            out = jnp.einsum('te,etd->td', onehot, y)
            return jnp.swapaxes(out.reshape(b, s, d), 0, 1)
        return _moe_forward(input_features, centroids, ln_g, ln_b, W1, b1, W2, b2)
    x = L0_attn_a_in_features
    x = x + _L0_attn_a_ref(_layernorm(x, axis=-1), L0_attn_a_q_proj_weight, L0_attn_a_k_proj_weight, L0_attn_a_v_proj_weight, L0_attn_a_o_proj_weight)
    x = x + _L0_ffn_ref(_layernorm(x, axis=-1), L0_ffn_Wqkv, L0_ffn_q_scale, L0_ffn_k_scale, L0_ffn_Wo, L0_ffn_ln_g, L0_ffn_ln_b, L0_ffn_W1, L0_ffn_b1, L0_ffn_W2, L0_ffn_b2)
    x = x + _L0_attn_b_ref(_layernorm(x, axis=-1), L0_attn_b_kernel)
    x = x + _L0_ffn_ref(_layernorm(x, axis=-1), L0_ffn_Wqkv, L0_ffn_q_scale, L0_ffn_k_scale, L0_ffn_Wo, L0_ffn_ln_g, L0_ffn_ln_b, L0_ffn_W1, L0_ffn_b1, L0_ffn_W2, L0_ffn_b2)
    x = x + _L1_attn_a_ref(_layernorm(x, axis=-1), L1_attn_a_key, L1_attn_a_value, L1_attn_a_in_proj_weight, L1_attn_a_out_weight)
    x = x + _L1_ffn_ref(_layernorm(x, axis=-1), L1_ffn_centroids, L1_ffn_ln_g, L1_ffn_ln_b, L1_ffn_W1, L1_ffn_b1, L1_ffn_W2, L1_ffn_b2)
    x = x + _L1_attn_b_ref(_layernorm(x, axis=-1), L1_attn_b_Wq, L1_attn_b_bq, L1_attn_b_Wk, L1_attn_b_bk, L1_attn_b_Wv, L1_attn_b_bv, L1_attn_b_Wp, L1_attn_b_bp)
    x = x + _L1_ffn_ref(_layernorm(x, axis=-1), L1_ffn_centroids, L1_ffn_ln_g, L1_ffn_ln_b, L1_ffn_W1, L1_ffn_b1, L1_ffn_W2, L1_ffn_b2)
    return x

_drawn_inputs = setup_inputs


def setup_inputs(seed=0):
    import zlib

    import numpy as np

    out = dict(_drawn_inputs(seed))
    spreads = {'L0_ffn_q_scale': (1.0, 0.535),
     'L0_ffn_k_scale': (1.0, 0.548),
     'L0_ffn_ln_g': (1.0, 0.587),
     'L0_ffn_ln_b': (0.0, 0.476),
     'L0_ffn_b1': (0.0, 0.1),
     'L0_ffn_b2': (0.0, 0.1),
     'L1_ffn_ln_g': (1.0, 0.2),
     'L1_ffn_ln_b': (0.0, 0.1)}
    factors = {'L1_attn_b_Wq': 8.0,
     'L1_attn_b_bq': 8.0,
     'L1_attn_b_Wk': 8.0,
     'L1_attn_b_bk': 64.0,
     'L1_attn_b_Wv': 7.904,
     'L1_attn_b_bv': 8.0,
     'L1_attn_b_Wp': 7.913,
     'L1_attn_b_bp': 4.068,
     'L1_ffn_b1': 8.0,
     'L1_ffn_b2': 5.298}
    for name, (base, spread) in spreads.items():
        noise = np.random.default_rng([zlib.crc32(name.encode()), seed]).standard_normal(out[name].shape)
        drawn = base * np.exp(spread * noise) if base else spread * noise
        out[name] = jnp.asarray(drawn.astype(out[name].dtype))
    for name, factor in factors.items():
        out[name] = (out[name] * factor).astype(out[name].dtype)
    return out
```

```python
from collections import namedtuple
from contextlib import ExitStack

import numpy as np

import concourse.bass as bass
from concourse import mybir

ALU = mybir.AluOpType
ACT = mybir.ActivationFunctionType
AX = mybir.AxisListType
F32 = mybir.dt.float32
F32R = mybir.dt.float32r
BF16 = mybir.dt.bfloat16
I32 = mybir.dt.int32

D = 128
B, T = 8, 256
N = B * T
NB = 512
NBLK = N // NB
DEPTH, HEADS, DH, WIN = 6, 16, 64, 32
NW = T // WIN
KW = 2 * WIN
GH = 4
G = HEADS // GH
UNITS = B * G
LOOP = 2 * G
F_IN = int(D * 4 * 2 / 3)
FC = [128, 128, F_IN - 256]
E_X, F_X = 8, 512
NEG = -1e30
LN_EPS = 1e-5
NAT = "natural_log_exp_and_others"


def rotary_tables():
    f4 = np.float32
    half = np.arange(0, DH, 2, dtype=f4)
    inv_freq = (f4(1.0) / np.power(f4(10000.0), half / f4(DH))).astype(f4)
    t = np.arange(T, dtype=f4)
    fr = (t[:, None] * inv_freq[None, :]).astype(f4)
    base = ((half + f4(0.4 * DH)) / f4(1.4 * DH)).astype(f4)
    power = ((t - T // 2) / f4(WIN // 2)).astype(f4)
    sc = np.power(base[None, :], power[:, None]).astype(f4)
    inv = (f4(1.0) / sc).astype(f4)
    cos, sin = np.cos(fr), np.sin(fr)
    r = np.arange(DH)
    freq = (r // 32) * 16 + r % 16
    sign = np.where(r % 32 < 16, f4(-1.0), f4(1.0)).astype(f4)
    out = np.zeros((D, 4, T), f4)
    for n, a in enumerate((cos * sc, sin * sc, cos * inv, sin * inv)):
        rows = a.T[freq]
        if n % 2:
            rows = rows * sign[:, None]
        out[:, n] = np.concatenate([rows, rows], 0)
    return out


def head_dims():
    r = np.arange(DH)
    return ((r % 32) // 16) * 32 + (r // 32) * 16 + r % 16


def window_mask():
    m = np.zeros((D, 2, GH, KW), np.float32)
    for p in range(D):
        for tile in range(2):
            i = tile * 128 + p
            w = i // WIN
            j = (w - 1) * WIN + np.arange(KW)
            m[p, tile, :, (i < j) | (i > j + WIN) | (j < 0)] = NEG
    return m.reshape(D, 2 * GH * KW)


def causal_mask():
    q = np.arange(T).reshape(2, 128).T[:, :, None]
    return np.where(np.arange(T)[None, None, :] > q, np.float32(NEG), np.float32(0)).reshape(D, 2 * T)


def head_scale_mask():
    m = np.zeros((D, 16), np.float32)
    for h in range(16):
        m[h * 8:h * 8 + 8, h] = 8.0 ** -0.5
    return m



class Parts:
    pass


def arena(M, shapes, at=0):
    views = []
    for name, shape in shapes.items():
        size = int(np.prod(shape))
        flat = M.arena[:, at:at + size]
        names = "abcdef"[:len(shape)]
        view = flat if len(shape) == 1 else flat.rearrange(
            f"p ({' '.join(names)}) -> p {' '.join(names)}", **dict(zip(names, shape)))
        views.append(view)
        at += size
    assert at <= M.arena.shape[1], (at, M.arena.shape)
    return namedtuple("Buffers", list(shapes))(*views)


def bank(M, i, n=512, rows=D):
    return M.ps[0:rows, i, 0:n]


def block_of(k):
    return slice(k * NB, (k + 1) * NB)


def enter_module(M, eng, m):
    if m.n == 0:
        eng.wait_ge(M.s.x_loaded, 16)
        eng.wait_ge(M.s.const_loaded, 16 * M.n_const)
        eng.wait_ge(M.s.const_set, 1)
        eng.wait_ge(M.s.ident_cast, 1)
    else:
        before = M.plan[m.n - 1]
        eng.wait_ge(before.end[0], before.end[1])
        if m.n == 1:
            eng.wait_ge(M.s.later_loaded, 16 * M.n_later)


def ln_pe(M, pe, src, n, shifted=None):
    s = M.s
    for k in range(NBLK):
        if shifted is not None:
            pe.wait_ge(s.ln_lo, shifted + k + 1)
            pe.wait_ge(s.ln_hi, shifted + k + 1)
        pe.matmul(bank(M, k), M.mean_w[:], src[:, block_of(k)], start=True, stop=True).then_inc(s.ln_mean, 1)
    for k in range(NBLK):
        pe.wait_ge(s.ln_squared, n + k + 1)
        pe.matmul(bank(M, 4 + k), M.mean_w[:], M.ln_sq[:, k, :], start=True, stop=True).then_inc(s.ln_var, 1)


def ln_act(M, act, n, shifted=None):
    s, nc = M.s, M.nc
    if shifted is not None:
        for k in range(NBLK):
            for j in range(2):
                o = k * NB + j * T
                ins = nc.scalar.copy(M.xc[64:128, o + 1:o + T], M.z[64:128, o:o + T - 1])
            ins.then_inc(s.ln_hi, 1)
    for k in range(NBLK):
        act.wait_ge(s.ln_centred, n + k + 1)
        nc.scalar.activation(M.ln_sq[:, k, :], M.xc[:, block_of(k)], ACT.Square).then_inc(s.ln_squared, 1)
    for k in range(NBLK):
        act.wait_ge(s.ln_var, n + k + 1)
        nc.scalar.activation(M.ln_rs[:, k, :], bank(M, 4 + k), ACT.Ln, bias=M.eps[:, 0:1]).then_inc(s.ln_log, 1)
        act.wait_ge(s.ln_log, n + k + 1)
        nc.scalar.activation(M.ln_rs[:, k, :], M.ln_rs[:, k, :], ACT.Exp, scale=-0.5).then_inc(s.ln_factor, 1)


def ln_dve(M, dve, src, dst, n, shifted=None, gain=None, shift=None):
    s, nc = M.s, M.nc
    if shifted is not None:
        for k in range(NBLK):
            nc.vector.tensor_copy(M.xc[0:64, block_of(k)], M.z[0:64, block_of(k)])
            first = M.xc[64:128, block_of(k)].rearrange("p (b t) -> p b t", t=T)[:, :, 0:1]
            nc.vector.memset(first, 0.0).then_inc(s.ln_lo, 1)
    for k in range(NBLK):
        dve.wait_ge(s.ln_mean, n + k + 1)
        nc.vector.tensor_tensor(M.xc[:, block_of(k)], src[:, block_of(k)], bank(M, k),
                                ALU.subtract).then_inc(s.ln_centred, 1)
    for k in range(NBLK):
        xc = M.xc[:, block_of(k)]
        dve.wait_ge(s.ln_factor, n + k + 1)
        if gain is None:
            nc.vector.tensor_tensor(dst[:, block_of(k)], xc, M.ln_rs[:, k, :], ALU.mult).then_inc(s.ln_out, 1)
        else:
            nc.vector.scalar_tensor_tensor(xc, xc, gain, M.ln_rs[:, k, :], ALU.mult,
                                           ALU.mult).then_inc(s.ln_gained, 1)
            dve.wait_ge(s.ln_gained, shifted + k + 1)
            nc.vector.tensor_scalar(xc, xc, shift, None, ALU.add).then_inc(s.ln_out, 1)


class Step:

    def __init__(self, eng, layer, s, n, batches, built, tok, first=False, last=False):
        self.eng, self.layer, self.s, self.n, self.batches, self.built, self.tok = eng, layer, s, n, batches, built, tok
        self.first, self.last = first, last

    def on(self, lag):
        return not (self.first and self.s < lag) and not (self.last and self.s - lag >= UNITS)

    def wait(self, sem, c):
        if not (self.first and c <= 0):
            self.eng.wait_ge(sem, self.n + c)


def unit_steps(M, eng, layer, step, tail):
    n, b8, b9 = eng.snap(layer * UNITS), eng.snap(layer * B), eng.snap(layer * (B + 1))
    for s in range(LOOP):
        step(M, Step(eng, layer, s, n, b8, b9, 0, first=True))
    with eng.Fori(1, UNITS // LOOP) as i:
        ni, b8i, b9i = eng.snap(n + i * LOOP), eng.snap(b8 + i * 2), eng.snap(b9 + i * 2)
        for s in range(LOOP):
            step(M, Step(eng, layer, s, ni, b8i, b9i, i * (2 * T)))
    for s in range(UNITS, UNITS + tail):
        step(M, Step(eng, layer, s, n, b8, b9, 0, last=True))


def stack_buffers(M):
    return arena(M, dict(tab=(2, 2, T), sh=(2, WIN + T), turned=(2, 4, T), swapped=(2, 4, T), sq=(4, T),
                         lg=(4, T), rn=(2, 4, T), q=(2, 2, T), kbd=(2, 2, 2, WIN + T), top=(8,), zs=(8, KW),
                         p=(8, KW), pt=(2, 2, 128), vbd=(NW, 2, 2, DH), total=(8,), inv=(8,), o=(8, DH),
                         ot=(2, T)))


def stack_hidden(M):
    return arena(M, dict(gate=(2, 3, NB), hid=(2, 3, NB)), at=4 * T + 2 * (WIN + T))


def pe_stack_step(M, st):
    pe, s, S, f, w = st.eng, st.s, M.st, stack_buffers(M), M.w
    scores, outs, turned, y = bank(M, 4), bank(M, 5), bank(M, 6), bank(M, 7, T)
    if st.on(2):
        u = s - 2
        st.wait(S.rotated, u + 1)
        st.wait(S.shifted, u)
        pe.matmul(scores, M.identb[:], M.wmask[:], start=True, stop=False, skip_group_check=True)
        sv = scores.rearrange("p (t h k) -> p t h k", t=2, h=2)
        for win in range(NW):
            c = 32 * (win % 4)
            for hp in range(2):
                last = pe.matmul(sv[c:c + 32, win // 4, hp, :], f.q[:, u % 2, hp, 32 * win:32 * win + 32],
                                 f.kbd[:, u % 2, hp, :, 32 * win:32 * win + KW], start=False, stop=True,
                                 skip_group_check=True)
        last.then_inc(S.scores, 1)
    if st.on(1):
        pe_stack_norms(M, st, 0)
    if st.on(3):
        u = s - 3
        st.wait(S.probs_taken, u + 1)
        st.wait(S.v1_taken, u + 1)
        st.wait(S.normed, u)
        ov = outs.rearrange("p (t h k) -> p t h k", t=2, h=2)
        for win in range(NW):
            c = 32 * (win % 4)
            for hp in range(2):
                last = pe.matmul(ov[c:c + 32, win // 4, hp, :], f.pt[:, win // 4, hp, c:c + 32],
                                 f.vbd[:, win, hp, :, :], start=True, stop=True)
        last.then_inc(S.outs, 1)
    if st.on(1):
        pe_stack_norms(M, st, 1)
    if st.on(0):
        u, g = s, s % G
        if g == 0:
            pe.wait_ge(S.tokens, st.built + (s // G + 1))
        st.wait(S.swapped, u)
        for qk in range(2):
            for hp in range(2):
                last = pe.matmul(bank(M, qk)[:, hp * T:hp * T + T], w.qk[:, qk, 2 * g + hp, :],
                                 f.sh[:, (s // G) % 2, WIN:WIN + T], start=True, stop=True)
        last.then_inc(S.qk, 1)
    if st.on(3):
        u = s - 3
        st.wait(S.normed, u + 1)
        st.wait(S.probs_taken, u + 1)
        ov = f.o.rearrange("p (t h) d -> p t h d", t=2)
        for hp in range(2):
            for tile in range(2):
                last = pe.transpose(turned[:, hp * T + tile * 128:hp * T + tile * 128 + 128],
                                    ov[:, tile, 2 * hp:2 * hp + 2, :], M.ident[:])
        last.then_inc(S.outs_turned, 1)
    if st.on(2):
        pe_stack_values(M, st, 0)
        u = s - 2
        st.wait(S.probs, u + 1)
        st.wait(S.outs_taken, u)
        pv = f.p.rearrange("p (t h) k -> p t h k", t=2)
        for tile in range(2):
            for hp in range(2):
                o = (2 * tile + hp) * 128
                last = pe.transpose(turned[:, o:o + 128], pv[:, tile, 2 * hp:2 * hp + 2, :], M.ident[:])
        last.then_inc(S.probs_turned, 1)
    if st.on(3):
        u = s - 3
        g = u % G
        st.wait(S.outs_taken, u + 1)
        if g == 0 and not (st.first and u // G == 0):
            pe.wait_ge(S.added, st.batches + u // G)
        for hp in range(2):
            last = pe.matmul(y, w.o[:, 2 * g + hp, :], f.ot[:, hp, :], start=(g == 0 and hp == 0),
                             stop=(g == G - 1 and hp == 1))
        last.then_inc(S.projected, 1)
    if st.on(2):
        pe_stack_values(M, st, 1)
    if st.first and s == 0:
        pe.wait_ge(S.tables, st.layer + 1)


def pe_stack_norms(M, st, qk):
    u, S = st.s - 1, M.st
    st.wait(S.k_rest if qk else S.q_rest, u + 1)
    if qk:
        st.wait(S.q_logged, u + 1)
    else:
        st.wait(S.k_logged, u)
    st.eng.matmul(bank(M, 2), M.half_ones[:], M.sq_hi[:, 2 * qk:2 * qk + 2, :], start=True, stop=False)
    st.eng.matmul(bank(M, 2), M.half_ones[:], M.sq_lo[:, 2 * qk:2 * qk + 2, :], start=False,
                  stop=True).then_inc(S.k_norms if qk else S.q_norms, 1)


def pe_stack_values(M, st, half):
    pe, S, f, w = st.eng, M.st, stack_buffers(M), M.w
    u = st.s - 2
    g, b = u % G, (u // G) % 2
    if half == 0:
        st.wait(S.v1_taken, u)
    else:
        st.wait(S.v0_taken, u + 1)
    vv = bank(M, 3).rearrange("p (w c) -> p w c", w=4)
    for w4 in range(4):
        win = 4 * half + w4
        keys = f.sh[:, b, 32 * win:32 * win + KW]
        for par in range(2):
            last = pe.matmul(vv[64 * par:64 * par + 64, w4, :], keys, w.v[:, par, 128 * g:128 * g + 128],
                             start=True, stop=True)
    last.then_inc(S.v1 if half else S.v0, 1)


def act_stack_step(M, st):
    s, S, f, nc = st.s, M.st, stack_buffers(M), M.nc
    turned = bank(M, 6)
    if st.on(1):
        act_stack_log(M, st, 0, S.q_norms, S.q_logged)
    if st.on(2):
        u = s - 2
        st.wait(S.shifted, u + 1)
        st.wait(S.probs_turned, u)
        st.wait(S.summed, u)
        nc.scalar.activation(f.p, f.zs, ACT.Exp, scale=8.0).then_inc(S.probs, 1)
    if st.on(1):
        u = s - 1
        act_stack_log(M, st, 1, S.k_norms, S.k_logged)
        st.wait(S.k_logged, u + 1)
        st.wait(S.rotated, u - 1)
        nc.scalar.activation(f.rn[:, u % 2, :, :], f.lg, ACT.Exp, scale=-0.5).then_inc(S.inverse_norms, 1)
    if st.on(0):
        st.wait(S.qk, s + 1)
        act_stack_squares(M, st, 0)
    if st.on(3):
        u = s - 3
        st.wait(S.outs_turned, u + 1)
        st.wait(S.projected, u)
        nc.scalar.copy(f.ot.rearrange("p h t -> p (h t)"), turned).then_inc(S.outs_taken, 1)
    if st.on(0):
        act_stack_upper(M, st, 0)
    if st.on(2):
        act_stack_values(M, st, 0)
    if st.on(0):
        act_stack_squares(M, st, 1)
        act_stack_upper(M, st, 1)
    if st.on(2):
        u = s - 2
        st.wait(S.probs_turned, u + 1)
        nc.scalar.copy(f.pt.rearrange("p t h k -> p (t h k)"), turned).then_inc(S.probs_taken, 1)
    if st.on(2):
        act_stack_values(M, st, 1)


def act_stack_squares(M, st, qk):
    S, f, nc, u = M.st, stack_buffers(M), M.nc, st.s
    st.wait(S.k_rest if qk else S.q_rest, u)
    nc.scalar.activation(f.sq[:, 2 * qk:2 * qk + 2, :].rearrange("p h t -> p (h t)"), bank(M, qk), ACT.Square)


def act_stack_upper(M, st, qk):
    S, nc, u = M.st, M.nc, st.s
    st.wait(S.k_norms if qk else S.q_norms, u)
    nc.scalar.activation(M.sq_hi[:, 2 * qk:2 * qk + 2, :].rearrange("p h t -> p (h t)"), bank(M, qk),
                         ACT.Square).then_inc(S.k_squared if qk else S.q_squared, 1)


def act_stack_values(M, st, half):
    S, f, u = M.st, stack_buffers(M), st.s - 2
    st.wait(S.v1 if half else S.v0, u + 1)
    if half == 0:
        st.wait(S.outs, u)
    vv = bank(M, 3).rearrange("p (w h d) -> p w h d", w=4, h=2)
    for par in range(2):
        r = slice(64 * par, 64 * par + 64)
        last = M.nc.scalar.copy(f.vbd[r, 4 * half:4 * half + 4, :, par, :], vv[r])
    last.then_inc(S.v1_taken if half else S.v0_taken, 1)


def act_stack_log(M, st, qk, norms, logged):
    st.wait(norms, st.s)
    M.nc.scalar.activation(stack_buffers(M).lg[:, 2 * qk:2 * qk + 2, :].rearrange("p h t -> p (h t)"), bank(M, 2),
                           ACT.Ln).then_inc(logged, 1)


def dve_stack_step(M, st):
    dve, s, S, f, nc = st.eng, st.s, M.st, stack_buffers(M), M.nc
    if st.on(2):
        u = s - 2
        sv = bank(M, 4).rearrange("p (h k) -> p h k", h=8)
        st.wait(S.scores, u + 1)
        nc.vector.tensor_reduce(f.top, sv, AX.X, ALU.max).then_inc(S.maxed, 1)
        st.wait(S.maxed, u + 1)
        st.wait(S.probs, u)
        nc.vector.tensor_tensor(f.zs, sv, f.top.unsqueeze(2).to_broadcast([D, 8, KW]),
                                ALU.subtract).then_inc(S.shifted, 1)
    if st.on(3):
        u = s - 3
        st.wait(S.outs, u + 1)
        st.wait(S.inverted, u + 1)
        st.wait(S.outs_turned, u)
        ov = bank(M, 5).rearrange("p (h d) -> p h d", h=8)
        nc.vector.tensor_tensor(f.o, ov, f.inv.unsqueeze(2).to_broadcast([D, 8, DH]),
                                ALU.mult).then_inc(S.normed, 1)
    if st.on(2):
        u = s - 2
        st.wait(S.probs, u + 1)
        nc.vector.tensor_reduce(f.total, f.p, AX.X, ALU.add).then_inc(S.summed, 1)
        st.wait(S.summed, u + 1)
        st.wait(S.normed, u)
        nc.vector.reciprocal(f.inv, f.total).then_inc(S.inverted, 1)
    if st.on(4) and s % G == 3:
        dve.wait_ge(S.projected, st.n + (s - 3))
        tok = st.tok + ((s - 4) // G) * T
        z = M.z[:, bass.ds(tok, T)]
        nc.vector.tensor_tensor(z, bank(M, 7, T), z, ALU.add).then_inc(S.added, 1)
    if st.on(1):
        u = s - 1
        st.wait(S.turned, u + 1)
        st.wait(S.inverse_norms, u + 1)
        st.wait(S.scores, u - 1)
        t, r = f.turned[:, u % 2], f.rn[:, u % 2]
        nc.vector.scalar_tensor_tensor(f.q[:, u % 2], r[:, 0:2], 1e12, t[:, 0:2], ALU.min, ALU.mult)
        for par in range(2):
            rows = slice(64 * par, 64 * par + 64)
            last = nc.vector.scalar_tensor_tensor(f.kbd[rows, u % 2, :, par, WIN:WIN + T], r[rows, 2:4], 1e12,
                                                  t[rows, 2:4], ALU.min, ALU.mult)
        last.then_inc(S.rotated, 1)
    if st.on(0):
        u = s
        for qk, squared in ((0, S.q_squared), (1, S.k_squared)):
            st.wait(squared, u + 1)
            rows = slice(2 * qk, 2 * qk + 2)
            nc.vector.tensor_tensor(f.turned[:, u % 2, rows], bank(M, qk).rearrange("p (h t) -> p h t", h=2),
                                    f.tab[:, qk, 0:1, :].to_broadcast([D, 2, T]), ALU.mult)
            last = nc.vector.stream_shuffle(f.swapped[:, u % 2, rows].rearrange("p h t -> p (h t)"),
                                            bank(M, qk), [(r + 16) % 32 for r in range(32)])
        last.then_inc(S.swapped, 1)


def pool_stack_tokens(M, pool, tok, buf):
    f, nc = stack_buffers(M), M.nc
    pool.sem_inc(M.s.pool_waited)
    nc.gpsimd.tensor_copy(f.sh[0:64, buf, WIN:WIN + T], M.z[0:64, bass.ds(tok, T)])
    nc.gpsimd.tensor_copy(f.sh[64:128, buf, WIN + 1:WIN + T],
                          M.z[64:128, bass.ds(tok, T - 1)]).then_inc(M.st.tokens, 1)


def pool_stack_step(M, st):
    pool, s, S, f, nc = st.eng, st.s, M.st, stack_buffers(M), M.nc
    if st.on(0) and s % G == 2 and not st.last:
        st.wait(S.v1, s - 2)
        st.wait(S.turned, s)
        pool_stack_tokens(M, pool, st.tok + (s // G + 1) * T, (s // G + 1) % 2)
        pool.wait_ge(S.tokens, st.built + (s // G + 2))
    if st.on(0):
        u = s
        for rows, squared, rest in ((slice(0, 2), S.q_squared, S.q_rest), (slice(2, 4), S.k_squared, S.k_rest)):
            st.wait(squared, u + 1)
            nc.gpsimd.tensor_tensor(M.sq_lo[:, rows, :], f.sq[:, rows, :], M.sq_hi[:, rows, :],
                                    ALU.subtract).then_inc(rest, 1)
        st.wait(S.swapped, u + 1)
        w = f.swapped[:, u % 2].rearrange("p (b h) t -> p b h t", b=2)
        nc.gpsimd.tensor_tensor(w, w, f.tab[:, :, 1, :].unsqueeze(2).to_broadcast([D, 2, 2, T]),
                                ALU.mult).then_inc(S.sined, 1)
        st.wait(S.sined, u + 1)
        nc.gpsimd.tensor_tensor(f.turned[:, u % 2], f.turned[:, u % 2], f.swapped[:, u % 2],
                                ALU.add).then_inc(S.turned, 1)


def pe_stack(M, pe, m):
    S, w, h = M.st, M.w, stack_hidden(M)
    pe.wait_ge(S.zeroed, m.k + 1)
    with pe.Fori(DEPTH * m.k, DEPTH * (m.k + 1)) as layer:
        pe.wait_ge(S.w_att, 16 * 4 * (layer + 1))
        unit_steps(M, pe, layer, pe_stack_step, 3)
        n4, n12 = pe.snap(layer * 4), pe.snap(layer * 12)
        ln_n = pe.snap(n4 + 4 * m.ln_inner)
        ln_pe(M, pe, M.xc, ln_n, shifted=n4)
        pe.wait_ge(S.w_ffn, 16 * 4 * (layer + 1))
        pe.wait_ge(M.s.ln_centred, ln_n + 4)
        for k in range(NBLK + 1):
            if k < NBLK:
                pe.wait_ge(M.s.ln_out, ln_n + k + 1)
                for half in (1, 0):
                    for c in range(3):
                        if k == 0 and half == 0 and c == 1:
                            pe.wait_ge(M.s.ln_log, ln_n + 2)
                        if k:
                            pe.wait_ge(S.gated if half else S.hidden, n12 + (3 * (k - 1) + c + 1))
                        o = half * F_IN + 128 * c
                        pe.matmul(bank(M, 3 * (1 - half) + c, rows=FC[c]), w.w1[:, o:o + FC[c]],
                                  M.xc[:, block_of(k)], start=True,
                                  stop=True).then_inc(S.gate_in if half else S.value_in, 1)
            if k >= 1:
                j = k - 1
                if j == 0:
                    pe.wait_ge(M.s.ln_log, ln_n + 4)
                pe.wait_ge(S.hidden, n12 + 3 * k)
                if j >= 2:
                    pe.wait_ge(S.state, n4 + (j - 1))
                for c in range(3):
                    last = pe.matmul(bank(M, 6 + j % 2), w.w2[0:FC[c], c, :], h.hid[0:FC[c], j % 2, c, :],
                                     start=(c == 0), stop=(c == 2))
                last.then_inc(S.ffn_out, 1)


def act_stack(M, act, m):
    S, w, nc, h = M.st, M.w, M.nc, stack_hidden(M)
    with act.Fori(DEPTH * m.k, DEPTH * (m.k + 1)) as layer:
        unit_steps(M, act, layer, act_stack_step, 3)
        n4, n8, n12 = act.snap(layer * 4), act.snap(layer * B), act.snap(layer * 12)
        act.wait_ge(S.added, n8 + B)
        ln_act(M, act, act.snap(n4 + 4 * m.ln_inner), shifted=n4)
        for k in range(NBLK):
            for c in range(3):
                act.wait_ge(S.gate_in, n12 + (3 * k + c + 1))
                if k >= 2:
                    act.wait_ge(S.hidden, n12 + (3 * (k - 2) + c + 1))
                r = slice(0, FC[c])
                nc.scalar.activation(h.gate[r, k % 2, c, :], bank(M, c, rows=FC[c]), ACT.Gelu,
                                     bias=w.b1[r, 3 + c:4 + c]).then_inc(S.gated, 1)
        nc.scalar.preload_act_table_set(NAT)
        act.wait_ge(S.state, n4 + 4)


def dve_stack(M, dve, m):
    S, w, nc, f, h = M.st, M.w, M.nc, stack_buffers(M), stack_hidden(M)
    for par in range(2):
        mine, other = slice(64 * par, 64 * par + 64), slice(64 - 64 * par, 128 - 64 * par)
        nc.vector.memset(f.kbd[other, :, :, par, :], 0.0)
        nc.vector.memset(f.kbd[mine, :, :, par, 0:WIN], 0.0)
    nc.vector.memset(f.vbd[0:64, :, :, 1, :], 0.0)
    nc.vector.memset(f.vbd[64:128, :, :, 0, :], 0.0).then_inc(S.zeroed, 1)
    with dve.Fori(DEPTH * m.k, DEPTH * (m.k + 1)) as layer:
        dve.wait_ge(S.w_att, 16 * 4 * (layer + 1))
        for qk in range(2):
            for cs in range(2):
                n = 2 * qk + cs
                last = nc.vector.tensor_scalar(f.tab[:, qk, cs, :], M.rot[:, n, :], w.scales[:, n:n + 1], None,
                                               ALU.mult)
        last.then_inc(S.tables, 1)
        dve.wait_ge(S.tables, layer + 1)
        unit_steps(M, dve, layer, dve_stack_step, 4)
        n4, n8, n12 = dve.snap(layer * 4), dve.snap(layer * B), dve.snap(layer * 12)
        dve.wait_ge(S.added, n8 + B)
        dve.wait_ge(S.w_ffn, 16 * 4 * (layer + 1))
        ln_dve(M, dve, M.xc, M.xc, dve.snap(n4 + 4 * m.ln_inner), shifted=n4, gain=w.vecs[:, 0:1],
               shift=w.vecs[:, 1:2])
        for k in range(NBLK + 1):
            if k < NBLK:
                for c in range(3):
                    dve.wait_ge(S.value_in, n12 + (3 * k + c + 1))
                    dve.wait_ge(S.gated, n12 + (3 * k + c + 1))
                    if k >= 2:
                        dve.wait_ge(S.ffn_out, n4 + (k - 1))
                    r = slice(0, FC[c])
                    nc.vector.scalar_tensor_tensor(h.hid[r, k % 2, c, :], bank(M, 3 + c, rows=FC[c]),
                                                   w.b1[r, c:c + 1], h.gate[r, k % 2, c, :], ALU.add,
                                                   ALU.mult).then_inc(S.hidden, 1)
            if k >= 1:
                j = k - 1
                dve.wait_ge(S.ffn_out, n4 + k)
                nc.vector.scalar_tensor_tensor(M.z[:, block_of(j)], bank(M, 6 + j % 2), w.vecs[:, 2:3],
                                               M.z[:, block_of(j)], ALU.add, ALU.add).then_inc(S.state, 1)
        dve.wait_ge(S.state, n4 + 4)
    for k in range(NBLK):
        last = nc.vector.tensor_tensor(M.x[:, block_of(k)], M.x[:, block_of(k)], M.z[:, block_of(k)], ALU.add)
    last.then_inc(S.residual, 1)


def pool_stack(M, pool, m):
    S, f, nc = M.st, stack_buffers(M), M.nc
    with pool.Fori(DEPTH * m.k, DEPTH * (m.k + 1)) as layer:
        nc.gpsimd.memset(f.sh[:, :, 0:WIN + 1], 0.0).then_inc(S.padded, 1)
        pool.wait_ge(S.padded, layer + 1)
        pool_stack_tokens(M, pool, 0, 0)
        pool.wait_ge(S.tokens, layer * (B + 1) + 1)
        pool.wait_ge(S.tables, layer + 1)
        unit_steps(M, pool, layer, pool_stack_step, 0)
        pool.wait_ge(S.state, layer * 4 + 4)


def sp_stack_attention(M, sp, layer):
    w, S, r = M.w, M.st, bass.ds(layer * D, D)
    for dst, name in ((w.qk, "stack_qk"), (w.v, "stack_v"), (w.scales, "stack_scales"), (w.o, "stack_o")):
        sp.dma_start(dst[:], M.ins[name][r]).then_inc(S.w_att, 16)


def sp_stack_hidden(M, sp, layer):
    w, S, r = M.w, M.st, bass.ds(layer * D, D)
    for dst, name in ((w.w1, "stack_w1"), (w.w2, "stack_w2"), (w.b1, "stack_b1"), (w.vecs, "stack_vecs")):
        sp.dma_start(dst[:], M.ins[name][r]).then_inc(S.w_ffn, 16)


def sp_stack(M, sp, m, more):
    S, first = M.st, DEPTH * m.k
    with sp.Fori(first, first + DEPTH - 1) as layer:
        sp.wait_ge(S.projected, (layer + 1) * UNITS)
        sp_stack_attention(M, sp, layer - first + 1)
        sp.wait_ge(S.state, (layer + 1) * 4)
        sp_stack_hidden(M, sp, layer - first + 1)
    if more:
        sp.wait_ge(S.projected, (first + DEPTH) * UNITS)
        sp_stack_attention(M, sp, 0)
        sp.wait_ge(S.state, (first + DEPTH) * 4)
        sp_stack_hidden(M, sp, 0)


def next_batch_step(m):
    return 12 if m.heads > 1 else 0


def mha_buffers(M):
    return arena(M, dict(tok=(T,), q=(T,), k=(2, T), qm=(2, 16, T), v=(2, 2, 16, 32), p=(3, 2, T), pt=(2, 2 * T),
                         ntop=(16, 2), total=(16, 2), inv=(16, 2), ot=(4, T), wraw=(4, D), sgn=(D,),
                         neg=(D,), wsum=(4,), wpad=(4, D), wt=(3, D), wo=(4, D)))


def pe_mha(M, pe, m):
    S, w, f, H = m.s, m.w, mha_buffers(M), m.heads
    ahead = next_batch_step(m)

    def project(done):
        pe.wait_ge(S.tok, done)
        for i, wt in ((0, w.q), (1, w.k)):
            pe.matmul(bank(M, 0)[:, i * T:i * T + T], wt, f.tok, start=True, stop=True)
        for t in range(2):
            o = bank(M, 1)[:, t * D:t * D + D]
            last = pe.matmul(o, f.tok[:, t * D:t * D + D], w.v, start=True, stop=not m.binary)
            if m.binary:
                last = pe.matmul(o, M.ones_row[:], w.bv, start=False, stop=True)
        last.then_inc(S.projected, 1)

    if m.binary:
        for i in range(3):
            pe.wait_ge(S.binarised, i + 1)
            pe.transpose(bank(M, 4)[:, i * D:i * D + D], f.wraw[:, i, :], M.ident[:]).then_inc(S.w_turned, 1)
        pe.wait_ge(S.binarised, 4)
        for i in range(4):
            last = pe.transpose(bank(M, 5)[:, i * D:i * D + D], f.wpad[:, i, :], M.ident[:])
        last.then_inc(S.w_turned, 1)
        pe.wait_ge(S.w_ready, 2)
    pe.wait_ge(S.zeroed, 1)
    project(1)
    pe.wait_ge(S.k, 1)
    pe.wait_ge(S.v, 1)
    with pe.Fori(0, B // 2) as pair:
        for par in range(2):
            b = pe.snap(pair * 2 + par)
            n, n4 = pe.snap(b * H), pe.snap(b * m.groups)
            for s in range(H + 3):
                if s < H:
                    h = s
                    if h % 4 == 0:
                        pe.wait_ge(S.q_masked, n4 + (h // 4 + 1))
                    if h >= 2:
                        pe.wait_ge(S.probs, n + (h - 1))
                    sv = bank(M, 2 + h % 2).rearrange("p (t k) -> p t k", t=2)
                    if m.causal:
                        pe.matmul(bank(M, 2 + h % 2), M.identb[:], M.cmask[:], start=True, stop=False,
                                  skip_group_check=True)
                    for t in range(2):
                        kw = 128 * (t + 1) if m.causal else T
                        last = pe.matmul(sv[:, t, 0:kw], f.qm[:, par, h, t * 128:t * 128 + 128], f.k[:, par, 0:kw],
                                         start=not m.causal, stop=True, skip_group_check=m.causal)
                    last.then_inc(S.scores, 1)
                if s == ahead:
                    project(b + 2)
                if 0 <= s - 2 < H:
                    h = s - 2
                    pe.wait_ge(S.normed, n + (h + 1))
                    if h >= 2:
                        pe.wait_ge(S.pt, n + (h - 1))
                    o = 0
                    for kt in range(2):
                        for qt in range(kt if m.causal else 0, 2):
                            last = pe.transpose(bank(M, 4 + h % 2)[:, o:o + 128],
                                                f.p[:, h % 3, qt, kt * 128:kt * 128 + 128], M.ident[:])
                            o += 128
                    last.then_inc(S.turned, 1)
                if 0 <= s - 3 < H:
                    h = s - 3
                    pe.wait_ge(S.pt, n + (h + 1))
                    if h == H - 1:
                        pe.wait_ge(S.k, b + 2)
                        pe.wait_ge(S.v, b + 2)
                    if h % 4 == 0 and h >= 8:
                        pe.wait_ge(S.outs, n4 + (h // 4 - 1))
                    c, wd = (32 * (h % 4), 32) if H > 1 else (0, D)
                    ob = bank(M, 6 + (h // 4) % 2, T)
                    for kt in range(2):
                        q0 = 128 * kt if m.causal else 0
                        val = f.v[:, par, kt, h, :] if H > 1 else f.v[:, par, kt].rearrange("p h e -> p (h e)")[:, 0:D]
                        last = pe.matmul(ob[c:c + wd, q0:T], val, f.pt[:, h % 2, kt * T:kt * T + T - q0],
                                         start=(kt == 0), stop=(kt == 1))
                    last.then_inc(S.pv, 1)
            if H > 1:
                pe.wait_ge(S.outs, n4 + 4)
                for i in range(4):
                    last = pe.matmul(bank(M, 0, T), w.o[:, i, :], f.ot[:, i, :], start=(i == 0), stop=(i == 3))
                last.then_inc(S.out_projected, 1)


def act_mha(M, act, m):
    S, w, f, H, nc = m.s, m.w, mha_buffers(M), m.heads, M.nc
    ahead = next_batch_step(m)

    def take(done, par):
        act.wait_ge(S.projected, done)
        pq = bank(M, 0)
        if m.binary:
            nc.scalar.activation(f.q, pq[:, 0:T], ACT.Identity, bias=w.bq).then_inc(S.q, 1)
            nc.scalar.activation(f.k[:, par], pq[:, T:2 * T], ACT.Identity, bias=w.bk).then_inc(S.k, 1)
        else:
            nc.scalar.copy(f.q, pq[:, 0:T]).then_inc(S.q, 1)
            nc.scalar.copy(f.k[:, par], pq[:, T:2 * T]).then_inc(S.k, 1)
        pv = bank(M, 1, T)
        if H > 1:
            nc.scalar.copy(f.v[:, par, :, :, 0:8], pv.rearrange("p (t h e) -> p t h e", t=2, h=16)).then_inc(S.v, 1)
        else:
            nc.scalar.copy(f.v[:, par].rearrange("p t h e -> p t (h e)")[:, :, 0:D],
                           pv.rearrange("p (t e) -> p t e", t=2)).then_inc(S.v, 1)

    if m.binary:
        for i in range(3):
            act.wait_ge(S.w_turned, i + 1)
        nc.scalar.copy(f.wt[:, 0:3, :].rearrange("p a b -> p (a b)"), bank(M, 4, 3 * D)).then_inc(S.w_ready, 1)
        act.wait_ge(S.w_turned, 4)
        nc.scalar.copy(w.o.rearrange("p a b -> p (a b)"), bank(M, 5)).then_inc(S.w_ready, 1)
    act.wait_ge(S.zeroed, 1)
    take(1, 0)
    with act.Fori(0, B // 2) as pair:
        for par in range(2):
            b = act.snap(pair * 2 + par)
            n = act.snap(b * H)
            for s in range(H + 3):
                if s < H:
                    h = s
                    act.wait_ge(S.maxed, n + (h + 1))
                    if h >= 3:
                        act.wait_ge(S.turned, n + (h - 2))
                    for t in range(2):
                        kw = 128 * (t + 1) if m.causal else T
                        last = nc.scalar.activation(f.p[:, h % 3, t, 0:kw],
                                                    bank(M, 2 + h % 2)[:, t * T:t * T + kw], ACT.Exp,
                                                    bias=f.ntop[:, h, t:t + 1], accum_out=f.total[:, h, t:t + 1])
                    last.then_inc(S.probs, 1)
                if s == ahead:
                    take(b + 2, 1 - par)
                if 0 <= s - 2 < H:
                    h = s - 2
                    wd = 384 if m.causal else 512
                    act.wait_ge(S.turned, n + (h + 1))
                    if h >= 2:
                        act.wait_ge(S.pv, n + (h - 1))
                    nc.scalar.copy(f.pt[:, h % 2, 0:wd], bank(M, 4 + h % 2, wd)).then_inc(S.pt, 1)


def dve_mha(M, dve, m):
    S, w, f, H, nc = m.s, m.w, mha_buffers(M), m.heads, M.nc
    if H > 1:
        nc.vector.memset(f.v.rearrange("p a t h e -> p (a t h e)"), 0.0)
    if m.binary:
        nc.vector.memset(f.wpad.rearrange("p a b -> p (a b)"), 0.0)
    nc.vector.memset(f.ntop.rearrange("p a b -> p (a b)"), 0.0).then_inc(S.zeroed, 1)
    if m.binary:
        dve.wait_ge(S.zeroed, 1)
        for i in range(4):
            raw = f.wraw[:, i, :]
            dve.wait_ge(S.w_raw, 16 * 4)
            if i:
                dve.wait_ge(S.binarised, i)
            nc.vector.tensor_reduce(f.wsum[:, i:i + 1], raw, AX.X, ALU.add,
                                    apply_absolute_value=True).then_inc(S.w_abs, 1)
            nc.vector.tensor_scalar(f.sgn, raw, 0.0, None, ALU.is_gt).then_inc(S.w_step, 1)
            nc.vector.tensor_scalar(f.neg, raw, 0.0, None, ALU.is_lt).then_inc(S.w_step, 1)
            dve.wait_ge(S.w_step, 5 * i + 2)
            nc.vector.tensor_tensor(f.sgn, f.sgn, f.neg, ALU.subtract).then_inc(S.w_step, 1)
            dve.wait_ge(S.w_step, 5 * i + 3)
            nc.vector.tensor_tensor(f.sgn, f.sgn, raw, ALU.subtract).then_inc(S.w_step, 1)
            dve.wait_ge(S.w_step, 5 * i + 4)
            nc.vector.tensor_tensor(f.sgn, raw, f.sgn, ALU.add).then_inc(S.w_step, 1)
            dve.wait_ge(S.w_step, 5 * i + 5)
            dve.wait_ge(S.w_abs, i + 1)
            if i < 3:
                o, src = raw, f.sgn
            else:
                o = f.wpad.rearrange("p i (j e) -> p i j e", j=4)[:, :, :, 0:8]
                src = f.sgn.rearrange("p (i j e) -> p i j e", i=4, j=4)
            nc.vector.tensor_scalar(o, src, f.wsum[:, i:i + 1], 1.0 / D, ALU.mult,
                                    ALU.mult).then_inc(S.binarised, 1)
    nc.vector.tensor_copy(f.tok, M.z[:, 0:T]).then_inc(S.tok, 1)
    with dve.Fori(0, B) as b:
        n = dve.snap(b * H)
        for s in range(H + 4):
            if s < H:
                h = s
                dve.wait_ge(S.scores, n + (h + 1))
                nc.vector.tensor_reduce(f.ntop[:, h, :], bank(M, 2 + h % 2).rearrange("p (t k) -> p t k", t=2),
                                        AX.X, ALU.max, negate=True).then_inc(S.maxed, 1)
            if s == (4 if H > 1 else 0):
                nc.vector.tensor_copy(f.tok, M.z[:, bass.ds(b * T + T, T)]).then_inc(S.tok, 1)
            if 0 <= s - 1 < H:
                h = s - 1
                dve.wait_ge(S.probs, n + (h + 1))
                nc.vector.reciprocal(f.inv[:, h, :], f.total[:, h, :]).then_inc(S.inverted, 1)
                dve.wait_ge(S.inverted, n + (h + 1))
                for t in range(2):
                    kw = 128 * (t + 1) if m.causal else T
                    p = f.p[:, h % 3, t, 0:kw]
                    last = nc.vector.tensor_scalar(p, p, f.inv[:, h, t:t + 1], None, ALU.mult)
                last.then_inc(S.normed, 1)
            if H > 1 and s >= 7 and (s - 7) % 4 == 0:
                i = (s - 7) // 4
                dve.wait_ge(S.pv, n + (4 * i + 4))
                nc.vector.tensor_copy(f.ot[:, i, :], bank(M, 6 + i % 2, T)).then_inc(S.outs, 1)
        x = M.x[:, bass.ds(b * T, T)]
        if H > 1:
            dve.wait_ge(S.out_projected, b + 1)
            y = bank(M, 0, T)
        else:
            dve.wait_ge(S.pv, n + 1)
            y = bank(M, 6, T)
        if m.binary:
            nc.vector.scalar_tensor_tensor(x, y, w.bp, x, ALU.add, ALU.add).then_inc(S.residual, 1)
        else:
            nc.vector.tensor_tensor(x, y, x, ALU.add).then_inc(S.residual, 1)
        dve.wait_ge(S.residual, b + 1)


def pool_mha(M, pool, m):
    S, f, H, nc = m.s, mha_buffers(M), m.heads, M.nc
    with pool.Fori(0, B // 2) as pair:
        for par in range(2):
            pool.wait_ge(S.q, pair * 2 + (par + 1))
            if H > 1:
                for i in range(4):
                    nc.gpsimd.tensor_tensor(f.qm[:, par, 4 * i:4 * i + 4, :], f.q.unsqueeze(1).to_broadcast([D, 4, T]),
                                            M.hmask[:, 4 * i:4 * i + 4].unsqueeze(2).to_broadcast([D, 4, T]),
                                            ALU.mult).then_inc(S.q_masked, 1)
            else:
                pool.sem_inc(M.s.pool_waited)
                nc.gpsimd.tensor_scalar(f.qm[:, par, 0, :], f.q, 0.125, None, ALU.mult).then_inc(S.q_masked, 1)


def lead_buffers(M):
    return arena(M, dict(qkv=(B, 3 * D), prod=(2, B * D), sc=(B, B, 16), pr=(B, B, 16), top=(B, 16),
                         tot=(B, 16), inv=(B, 16), att=(B, D), at=(4 * D,)))


def pe_lead(M, pe, m):
    S, w, f = m.s, m.w, lead_buffers(M)
    for t in range(2):
        for s in range(B):
            j = t * B + s
            if j >= 4:
                pe.wait_ge(S.qkv, j - 3)
            o = s * T + t * 128
            pe.matmul(bank(M, j % 4, 3 * D), M.z[:, o:o + 128], w.qkv, start=True,
                      stop=True).then_inc(S.projected, 1)
        for half in range(2):
            pe.wait_ge(S.att, t * B + 4 * half + 4)
            i = 2 * t + half
            for s in range(4):
                last = pe.transpose(bank(M, 4 + i % 2)[:, s * D:s * D + D], f.att[:, 4 * half + s, :], M.ident[:])
            last.then_inc(S.turned, 1)
            pe.wait_ge(S.at, i + 1)
            if i >= 2:
                pe.wait_ge(S.residual, i - 1)
            pe.matmul(bank(M, 6 + i % 2), w.o, f.at, start=True, stop=True).then_inc(S.out_projected, 1)


def act_lead(M, act, m):
    S, f, nc = m.s, lead_buffers(M), M.nc
    for t in range(2):
        if t == 1:
            act.wait_ge(S.att, B)
        for s in range(B):
            j = t * B + s
            act.wait_ge(S.projected, j + 1)
            nc.scalar.copy(f.qkv[:, s, :], bank(M, j % 4, 3 * D)).then_inc(S.qkv, 1)
        act.wait_ge(S.shifted, t + 1)
        nc.scalar.activation(f.pr.rearrange("p a b c -> p (a b c)"), f.pr.rearrange("p a b c -> p (a b c)"),
                             ACT.Exp, scale=8.0 ** -0.5).then_inc(S.exped, 1)
        for half in range(2):
            i = 2 * t + half
            act.wait_ge(S.turned, i + 1)
            if i >= 1:
                act.wait_ge(S.out_projected, i)
            nc.scalar.copy(f.at, bank(M, 4 + i % 2)).then_inc(S.at, 1)


def dve_lead(M, dve, m):
    S, f, nc = m.s, lead_buffers(M), M.nc
    for t in range(2):
        for s in range(B):
            j = 2 * t * B + s
            dve.wait_ge(S.prod, j + 1)
            nc.vector.tensor_reduce(f.sc[:, s].rearrange("p t h -> p (t h)"),
                                    f.prod[:, j % 2, :].rearrange("p (a e) -> p a e", e=8), AX.X,
                                    ALU.add).then_inc(S.reduced, 1)
        dve.wait_ge(S.reduced, (t + 1) * B)
        by_key = f.sc.rearrange("p s t h -> p s h t")
        nc.vector.tensor_reduce(f.top, by_key, AX.X, ALU.max).then_inc(S.step, 1)
        dve.wait_ge(S.step, 4 * t + 1)
        nc.vector.tensor_tensor(f.pr, f.sc, f.top.unsqueeze(2).to_broadcast([D, B, B, 16]),
                                ALU.subtract).then_inc(S.shifted, 1)
        dve.wait_ge(S.exped, t + 1)
        nc.vector.tensor_reduce(f.tot, f.pr.rearrange("p s t h -> p s h t"), AX.X, ALU.add).then_inc(S.step, 1)
        dve.wait_ge(S.step, 4 * t + 2)
        nc.vector.reciprocal(f.inv, f.tot).then_inc(S.step, 1)
        dve.wait_ge(S.step, 4 * t + 3)
        nc.vector.tensor_tensor(f.pr, f.pr, f.inv.unsqueeze(2).to_broadcast([D, B, B, 16]),
                                ALU.mult).then_inc(S.step, 1)
        for s in range(B):
            j = (2 * t + 1) * B + s
            dve.wait_ge(S.prod, j + 1)
            if s % 4 == 0 and t == 1:
                dve.wait_ge(S.turned, s // 4 + 1)
            nc.vector.tensor_reduce(f.att[:, s, :], f.prod[:, j % 2, :].rearrange("p (t c) -> p c t", t=B),
                                    AX.X, ALU.add).then_inc(S.att, 1)
        for half in range(2):
            i = 2 * t + half
            dve.wait_ge(S.out_projected, i + 1)
            x = M.x[:].rearrange("p (s t) -> p s t", s=B)[:, 4 * half:4 * half + 4, t * 128:t * 128 + 128]
            nc.vector.tensor_tensor(x, bank(M, 6 + i % 2).rearrange("p (s t) -> p s t", s=4), x,
                                    ALU.add).then_inc(S.residual, 1)


def pool_lead(M, pool, m):
    S, f, nc = m.s, lead_buffers(M), M.nc
    for t in range(2):
        pool.wait_ge(S.qkv, (t + 1) * B)
        for s in range(B):
            j = 2 * t * B + s
            if s >= 2:
                pool.wait_ge(S.reduced, t * B + s - 1)
            elif t:
                pool.wait_ge(S.att, t * B)
            q = f.qkv[:, s, 0:D].unsqueeze(1).to_broadcast([D, B, D])
            nc.gpsimd.tensor_tensor(f.prod[:, j % 2, :].rearrange("p (t c) -> p t c", t=B), q,
                                    f.qkv[:, :, D:2 * D], ALU.mult).then_inc(S.prod, 1)
        pool.wait_ge(S.step, 4 * t + 4)
        for s in range(B):
            j = (2 * t + 1) * B + s
            if s >= 2:
                pool.wait_ge(S.att, t * B + s - 1)
            pr = f.pr[:, s].unsqueeze(3).to_broadcast([D, B, 16, 8])
            nc.gpsimd.tensor_tensor(f.prod[:, j % 2, :].rearrange("p (t h e) -> p t h e", t=B, h=16), pr,
                                    f.qkv[:, :, 2 * D:3 * D].rearrange("p t (h e) -> p t h e", h=16),
                                    ALU.mult).then_inc(S.prod, 1)


def moe_buffers(M):
    return arena(M, dict(xe=(2, NB), hid=(2, 4, NB), lg=(16, E_X), top=(16,), eq=(16, E_X), rank=(16, E_X),
                         rtop=(16,), one=(16, E_X), oneT=(N,)))


def pe_moe(M, pe, m):
    S, w, f = M.mo, M.w, moe_buffers(M)
    gate = bank(M, 7, 16 * E_X).rearrange("p (t e) -> p t e", e=E_X)
    for t in range(16):
        last = pe.matmul(gate[:, t, :], M.z[:, t * 128:t * 128 + 128], w.cent[:], start=True, stop=True)
    last.then_inc(S.logits, 1)
    ln_pe(M, pe, M.z, 4 * m.ln_inner)
    pe.wait_ge(S.one_hot, m.k + 1)
    pe.wait_ge(M.s.ln_out, 4 * m.ln_inner + 4)
    for t in range(16):
        last = pe.transpose(M.ps[0:E_X, t // 4, (t % 4) * 128:(t % 4) * 128 + 128], f.one[:, t, :], M.ident[:])
    last.then_inc(S.one_turned, 1)
    pe.wait_ge(S.one_taken, m.k + 1)
    pe.wait_ge(S.not_mine, m.k + 1)
    with pe.Fori(NBLK * m.k, NBLK * (m.k + 1)) as blk:
        n8 = pe.snap(blk * E_X)
        tok = (blk - NBLK * m.k) * NB
        y = bank(M, 4)
        pe.matmul(y, w.b2[:], f.oneT[0:E_X, bass.ds(tok, NB)], start=True, stop=False)
        for e in range(E_X + 1):
            if e < E_X:
                pe.wait_ge(S.normed, n8 + (e + 1))
                for c in range(4):
                    if e and c % 2 == 0:
                        pe.wait_ge(S.relu_a if c == 0 else S.relu_v, n8 + e)
                    pe.matmul(bank(M, c), w.m1[:, e, 128 * c:128 * c + 128], f.xe[:, e % 2, :],
                              start=True, stop=False)
                    last = pe.matmul(bank(M, c), w.pick[:, e, :], w.other[:, bass.ds(tok, NB)],
                                     start=False, stop=True)
                    if c % 2:
                        last.then_inc(S.first_a if c == 1 else S.first_v, 1)
            if e >= 1:
                j = e - 1
                pe.wait_ge(S.relu_a, n8 + e)
                pe.wait_ge(S.relu_v, n8 + e)
                for c in range(4):
                    last = pe.matmul(y, w.m2[:, j, c, :], f.hid[:, j % 2, c, :], start=False,
                                     stop=(e == E_X and c == 3))
                last.then_inc(S.second, 1)
        pe.wait_ge(S.residual, blk + 1)


def act_moe(M, act, m):
    S, w, f, nc = M.mo, M.w, moe_buffers(M), M.nc
    ln_act(M, act, 4 * m.ln_inner)
    act.wait_ge(S.one_turned, m.k + 1)
    nc.scalar.copy(f.oneT[0:E_X, :], M.ps[0:E_X, 0:4, :].rearrange("p b t -> p (b t)")).then_inc(S.one_taken, 1)
    with act.Fori(NBLK * m.k, NBLK * (m.k + 1)) as blk:
        n8 = act.snap(blk * E_X)
        for e in range(E_X):
            act.wait_ge(S.first_a, n8 + (e + 1))
            if e >= 2:
                act.wait_ge(S.second, n8 + (e - 1))
            for c in range(2):
                last = nc.scalar.activation(f.hid[:, e % 2, c, :], bank(M, c), ACT.Relu,
                                            bias=w.mb1[:, e, c:c + 1])
            last.then_inc(S.relu_a, 1)
        act.wait_ge(S.second, n8 + E_X)


def dve_moe(M, dve, m):
    S, w, f, nc, k = M.mo, M.w, moe_buffers(M), M.nc, m.k
    shape = [D, 16, E_X]
    gate = bank(M, 7, 16 * E_X).rearrange("p (t e) -> p t e", e=E_X)
    ranks = M.w.ranks[:].unsqueeze(1).to_broadcast(shape)
    dve.wait_ge(S.logits, k + 1)
    nc.vector.tensor_copy(f.lg, gate).then_inc(S.pick, 1)
    dve.wait_ge(S.pick, 5 * k + 1)
    nc.vector.tensor_reduce(f.top, f.lg, AX.X, ALU.max).then_inc(S.pick, 1)
    dve.wait_ge(S.pick, 5 * k + 2)
    nc.vector.tensor_tensor(f.eq, f.lg, f.top.unsqueeze(2).to_broadcast(shape), ALU.is_ge).then_inc(S.pick, 1)
    dve.wait_ge(S.pick, 5 * k + 3)
    nc.vector.tensor_tensor(f.rank, f.eq, ranks, ALU.mult).then_inc(S.pick, 1)
    dve.wait_ge(S.pick, 5 * k + 4)
    nc.vector.tensor_reduce(f.rtop, f.rank, AX.X, ALU.max).then_inc(S.pick, 1)
    dve.wait_ge(S.pick, 5 * k + 5)
    nc.vector.tensor_tensor(f.one, f.rank, f.rtop.unsqueeze(2).to_broadcast(shape),
                            ALU.is_equal).then_inc(S.one_hot, 1)
    ln_dve(M, dve, M.z, M.xc, 4 * m.ln_inner)
    dve.wait_ge(S.one_taken, k + 1)
    nc.vector.tensor_scalar(w.other[:], f.oneT[0:E_X, :], -1.0, 1.0, ALU.mult, ALU.add).then_inc(S.not_mine, 1)
    dve.wait_ge(M.s.ln_out, 4 * m.ln_inner + 4)
    with dve.Fori(NBLK * k, NBLK * (k + 1)) as blk:
        n8 = dve.snap(blk * E_X)
        tok = (blk - NBLK * k) * NB

        def norm(e):
            nc.vector.tensor_scalar(f.xe[:, e % 2, :], M.xc[:, bass.ds(tok, NB)], w.mg[:, e:e + 1],
                                    w.mb[:, e:e + 1], ALU.mult, ALU.add).then_inc(S.normed, 1)
        norm(0)
        norm(1)
        for e in range(E_X):
            dve.wait_ge(S.first_v, n8 + (e + 1))
            if e + 2 < E_X:
                norm(e + 2)
            if e >= 2:
                dve.wait_ge(S.second, n8 + (e - 1))
            for c in range(2, 4):
                last = nc.vector.tensor_scalar(f.hid[:, e % 2, c, :], bank(M, c), w.mb1[:, e, c:c + 1], 0.0,
                                               ALU.add, ALU.max)
            last.then_inc(S.relu_v, 1)
        dve.wait_ge(S.second, n8 + E_X)
        x, z = M.x[:, bass.ds(tok, NB)], M.z[:, bass.ds(tok, NB)]
        nc.vector.tensor_tensor(z, bank(M, 4), z, ALU.add).then_inc(S.with_input, 1)
        dve.wait_ge(S.with_input, blk + 1)
        nc.vector.tensor_tensor(x, x, z, ALU.add).then_inc(S.residual, 1)


def pe_program(M, pe):
    for m in M.plan:
        enter_module(M, pe, m)
        ln_pe(M, pe, M.x, 4 * m.ln_outer)
        pe.wait_ge(M.s.ln_out, 4 * m.ln_outer + 4)
        {"stack": pe_stack, "mha": pe_mha, "lead": pe_lead, "moe": pe_moe}[m.kind](M, pe, m)


def act_program(M, act):
    for m in M.plan:
        enter_module(M, act, m)
        M.nc.scalar.preload_act_table_set(NAT)
        ln_act(M, act, 4 * m.ln_outer)
        {"stack": act_stack, "mha": act_mha, "lead": act_lead, "moe": act_moe}[m.kind](M, act, m)


def dve_program(M, dve):
    nc = M.nc
    nc.vector.memset(M.mean_w[:], 1.0 / D)
    for r in (0, 64):
        for c in (0, 64):
            nc.vector.memset(M.half_ones[r:r + 64, c:c + 64].bitcast(F32), 1.0 if r == c else 0.0)
    nc.vector.memset(M.ones_row[:], 1.0)
    nc.vector.memset(M.z[:, N:N + T], 0.0)
    nc.vector.memset(M.eps[:], LN_EPS).then_inc(M.s.const_set, 1)
    dve.wait_ge(M.s.const_loaded, 16 * M.n_const)
    nc.vector.tensor_copy(M.identb[:], M.ident[:])
    nc.vector.tensor_copy(M.wmask[:], M.mask_in[:, 0, :])
    nc.vector.tensor_copy(M.cmask[:], M.mask_in[:, 1, :])
    nc.vector.tensor_copy(M.w.pick[:].rearrange("p a b -> p (a b)"), M.pick_in).then_inc(M.s.ident_cast, 1)
    for m in M.plan:
        enter_module(M, dve, m)
        ln_dve(M, dve, M.x, M.z, 4 * m.ln_outer)
        dve.wait_ge(M.s.ln_out, 4 * m.ln_outer + 4)
        {"stack": dve_stack, "mha": dve_mha, "lead": dve_lead, "moe": dve_moe}[m.kind](M, dve, m)


def pool_program(M, pool):
    for m in M.plan:
        if m.kind == "moe":
            continue
        enter_module(M, pool, m)
        pool.wait_ge(M.s.ln_out, 4 * m.ln_outer + 4)
        {"stack": pool_stack, "mha": pool_mha, "lead": pool_lead}[m.kind](M, pool, m)


def sp_program(M, sp):
    ins, w = M.ins, M.w
    sp.dma_start(M.x[:], ins["x"]).then_inc(M.s.x_loaded, 16)
    for dst, src in M.constants:
        sp.dma_start(dst, src).then_inc(M.s.const_loaded, 16)
    for dst, src in M.later_constants:
        sp.dma_start(dst, src).then_inc(M.s.later_loaded, 16)
    if any(m.kind == "stack" for m in M.plan):
        sp_stack_attention(M, sp, 0)
        sp_stack_hidden(M, sp, 0)
    for m in M.plan:
        if m.kind == "stack":
            sp_stack(M, sp, m, any(o.kind == "stack" for o in M.plan[m.n + 1:]))
        if m.kind == "mha" and m.binary:
            enter_module(M, sp, m)
            for i, name in enumerate(("Wq", "Wk", "Wv", "Wp")):
                sp.dma_start(mha_buffers(M).wraw[:, i, :], ins["L1_attn_b_" + name]).then_inc(m.s.w_raw, 16)
    end = M.plan[-1].end
    sp.wait_ge(end[0], end[1])
    sp.dma_start(M.out, M.x[:]).then_inc(M.s.stored, 16)
    sp.wait_ge(M.s.stored, 16)


STACK_SIGNALS = """w_att w_ffn tables zeroed padded tokens qk q_squared k_squared q_norms k_norms q_rest k_rest q_logged k_logged
 inverse_norms swapped sined turned rotated scores maxed shifted probs summed inverted probs_turned probs_taken
 v0 v1 v0_taken v1_taken outs normed outs_turned outs_taken projected added gate_in value_in gated hidden
 ffn_out state residual"""
MHA_SIGNALS = """zeroed tok projected q k v q_masked scores maxed probs inverted normed turned pt pv outs
 out_projected residual"""
BINARY_SIGNALS = "w_raw w_abs w_step binarised w_turned w_ready"
LEAD_SIGNALS = "projected qkv prod reduced step shifted exped att turned at out_projected residual"
MOE_SIGNALS = """logits pick one_hot one_turned one_taken not_mine normed first_a first_v relu_a relu_v second
 with_input residual"""
SHARED_SIGNALS = """x_loaded const_loaded later_loaded const_set ident_cast stored ln_lo ln_hi ln_mean ln_centred ln_squared
 ln_var ln_log ln_factor ln_gained ln_out pool_waited"""
MODULES = ("causal", "stack", "single", "stack", "lead", "moe", "binary", "moe")


def signals(sem, prefix, names):
    return namedtuple("Signals", names.split())(*[sem(f"{prefix}_{n}") for n in names.split()])


def hybrid_program(nc, ins, out_ap, modules=MODULES):
    with ExitStack() as ctx:
        def sb(name, shape, dt=F32):
            return ctx.enter_context(nc.sbuf_tensor(name, shape, dt))

        def sem(name):
            return ctx.enter_context(nc.semaphore(name))

        M = Parts()
        M.nc, M.ins, M.out = nc, ins, out_ap
        M.ps = ctx.enter_context(nc.psum_tensor("banks", [D, 8, 512], F32))
        M.x = sb("x", [D, N])
        M.z = sb("z", [D, N + T])
        M.xc = sb("xc", [D, N])
        M.ident, M.identb = sb("ident", [D, D]), sb("identb", [D, D], BF16)
        M.mean_w, M.half_ones = sb("mean_w", [D, D]), sb("half_ones", [D, D], F32R)
        M.ones_row, M.eps, M.hmask = sb("ones_row", [1, D]), sb("eps", [D, 1]), sb("hmask", [D, 16])
        M.rot = sb("rot", [D, 4, T])
        M.wmask, M.cmask = sb("wmask", [D, 512], BF16), sb("cmask", [D, 512], BF16)
        M.ln_sq, M.ln_rs = sb("ln_sq", [D, NBLK, NB]), sb("ln_rs", [D, NBLK, NB])
        M.sq_hi, M.sq_lo = sb("sq_hi", [D, 4, T], F32R), sb("sq_lo", [D, 4, T], F32R)
        M.arena = sb("arena", [D, 17760])
        M.mask_in = M.arena[:, 0:1024].rearrange("p (a b) -> p a b", a=2)
        M.pick_in = M.arena[0:E_X, 1024:1024 + E_X * D]

        M.w = w = Parts()
        w.qk, w.v, w.scales = sb("w_qk", [D, 2, 8, D]), sb("w_v", [D, 2, 512]), sb("w_scales", [D, 4])
        w.o, w.w1, w.w2 = sb("w_o", [D, 8, D]), sb("w_w1", [D, 2 * F_IN]), sb("w_w2", [D, 3, D])
        w.b1, w.vecs = sb("w_b1", [D, 6]), sb("w_vecs", [D, 3])
        w.cent, w.m1, w.m2 = sb("w_cent", [D, E_X]), sb("w_m1", [D, E_X, F_X]), sb("w_m2", [D, E_X, 4, D])
        w.mb1, w.mg, w.mb = sb("w_mb1", [D, E_X, 4]), sb("w_mg", [D, E_X]), sb("w_mb", [D, E_X])
        w.b2, w.ranks = sb("w_b2", [E_X, D]), sb("w_ranks", [D, E_X])
        w.pick, w.other = sb("w_pick", [E_X, E_X, D], BF16), sb("w_other", [E_X, N], BF16)
        causal, single, lead, binary = Parts(), Parts(), Parts(), Parts()
        causal.qkv, causal.o = sb("c_qkv", [D, 3, D]), sb("c_o", [D, 4, D])
        single.qkv = sb("s_qkv", [D, 3, D])
        lead.qkv, lead.o = sb("l_qkv", [D, 3 * D]), sb("l_o", [D, D])
        binary.b, binary.bv = sb("b_bias", [D, 3]), sb("b_v", [1, D])
        for v in (causal, single):
            v.q, v.k, v.v = (v.qkv[:, i, :] for i in range(3))
        causal.o = causal.o[:]
        lead.qkv, lead.o = lead.qkv[:], lead.o[:]
        f = mha_buffers(M)
        binary.q, binary.k, binary.v, binary.o = f.wt[:, 0, :], f.wt[:, 1, :], f.wt[:, 2, :], f.wo
        binary.bq, binary.bk, binary.bp = (binary.b[:, i:i + 1] for i in range(3))
        binary.bv = binary.bv[:]
        M.constants = [(M.ident[:], ins["ident"]), (M.mask_in[:, 0, :], ins["wmask"]),
                       (M.mask_in[:, 1, :], ins["cmask"]), (M.pick_in, ins["pick"]), (M.hmask[:], ins["hmask"]),
                       (causal.qkv[:], ins["c_qkv"]), (causal.o, ins["c_o"])]
        M.later_constants = [(M.rot[:], ins["rot"]), (single.qkv[:], ins["s_qkv"]), (lead.qkv, ins["l_qkv"]),
                             (lead.o, ins["l_o"]), (binary.b[:], ins["b_bias"]), (binary.bv, ins["b_v"]),
                             (w.cent[:], ins["cent"]), (w.mb1[:], ins["m_b1"]), (w.mg[:], ins["m_g"]),
                             (w.mb[:], ins["m_b"]), (w.b2[:], ins["L1_ffn_b2"]), (w.ranks[:], ins["ranks"]),
                             (w.m1[:], ins["m_w1"]), (w.m2[:], ins["m_w2"])]
        M.n_const, M.n_later = len(M.constants), len(M.later_constants)

        M.s = signals(sem, "all", SHARED_SIGNALS)
        M.plan, norms, calls = [], 0, {"stack": 0, "moe": 0}
        for n, name in enumerate(modules):
            m = Parts()
            m.n, m.name, m.ln_outer, m.k, m.binary = n, name, norms, calls.get(name, 0), name == "binary"
            norms += 1
            if name == "stack":
                M.st = M.st if m.k else signals(sem, "stack", STACK_SIGNALS)
                m.kind, m.end, m.ln_inner = "stack", (M.st.residual, m.k + 1), norms - DEPTH * m.k
                norms += DEPTH
                calls[name] += 1
            elif name == "moe":
                M.mo = M.mo if m.k else signals(sem, "moe", MOE_SIGNALS)
                m.kind, m.end, m.ln_inner = "moe", (M.mo.residual, NBLK * (m.k + 1)), norms
                norms += 1
                calls[name] += 1
            elif name == "lead":
                m.kind, m.s, m.w = "lead", signals(sem, name, LEAD_SIGNALS), lead
                m.end = (m.s.residual, 4)
            else:
                m.kind, m.causal, m.heads = "mha", name == "causal", 1 if name == "single" else 16
                m.groups = max(1, m.heads // 4)
                m.s = signals(sem, name, MHA_SIGNALS + (" " + BINARY_SIGNALS if m.binary else ""))
                m.w = {"causal": causal, "single": single, "binary": binary}[name]
                m.end = (m.s.residual, B)
            M.plan.append(m)

        block = ctx.enter_context(nc.Block())

        @block.sync
        def _(sp):
            sp_program(M, sp)

        @block.gpsimd
        def _(pool):
            pool_program(M, pool)

        @block.scalar
        def _(act):
            act_program(M, act)

        @block.vector
        def _(dve):
            dve_program(M, dve)

        @block.tensor
        def _(pe):
            pe_program(M, pe)


def laid_out(a):
    order = head_dims()
    cols = (np.arange(HEADS)[:, None] * DH + order[None, :]).reshape(-1)
    wqkv = a["L0_ffn_Wqkv"]
    inner = HEADS * DH
    qk = np.stack([wqkv[:, :, cols], wqkv[:, :, inner + cols]], 2).reshape(DEPTH * D, 2, 8, D)
    v = wqkv[:, :, 2 * inner:].reshape(DEPTH, D, 8, 2, DH).transpose(0, 1, 3, 2, 4).reshape(DEPTH * D, 2, 512)
    half = (order + 32) % DH
    qs, ks = a["L0_ffn_q_scale"], a["L0_ffn_k_scale"]
    scales = np.stack([np.tile(s, (1, 2)) for s in (qs[:, order], qs[:, half], ks[:, order], ks[:, half])], 2)
    rows = np.minimum(np.arange(3 * D), F_IN - 1)
    b1 = a["L0_ffn_b1"]
    hid = np.concatenate([b1[:, rows].reshape(DEPTH, 3, D), b1[:, F_IN + rows].reshape(DEPTH, 3, D)], 1)
    heads = np.arange(16)
    w_o = a["L0_attn_a_o_proj_weight"].T
    c_o = np.zeros((D, 4, D), np.float32)
    for h in heads:
        c_o[32 * (h % 4):32 * (h % 4) + 8, h // 4] = w_o[8 * h:8 * h + 8]
    pick = np.zeros((E_X, E_X, D), np.float32)
    pick[np.arange(E_X), np.arange(E_X)] = NEG
    return {
        "x": a["L0_attn_a_in_features"].reshape(N, D).T,
        "ident": np.eye(D, dtype=np.float32), "wmask": window_mask(), "cmask": causal_mask(),
        "pick": pick.reshape(E_X, E_X * D), "hmask": head_scale_mask(), "rot": rotary_tables(),
        "ranks": np.tile(np.arange(E_X, 0, -1, dtype=np.float32), (D, 1)),
        "c_qkv": np.stack([a[f"L0_attn_a_{n}_proj_weight"].T for n in "qkv"], 1), "c_o": c_o,
        "s_qkv": a["L0_attn_b_kernel"].transpose(1, 0, 2),
        "l_qkv": a["L1_attn_a_in_proj_weight"].T.reshape(D, 16, 3, 8).transpose(0, 2, 1, 3).reshape(D, 3 * D),
        "l_o": a["L1_attn_a_out_weight"].T,
        "b_bias": np.stack([a["L1_attn_b_bq"], a["L1_attn_b_bk"], a["L1_attn_b_bp"]], 1),
        "b_v": a["L1_attn_b_bv"][None, :],
        **{f"L1_attn_b_{n}": a[f"L1_attn_b_{n}"] for n in ("Wq", "Wk", "Wv", "Wp")},
        "cent": a["L1_ffn_centroids"].T, "m_w1": a["L1_ffn_W1"].transpose(1, 0, 2),
        "m_w2": a["L1_ffn_W2"].reshape(E_X, 4, D, D).transpose(2, 0, 1, 3),
        "m_b1": a["L1_ffn_b1"].reshape(E_X, 4, D).transpose(2, 0, 1),
        "m_g": a["L1_ffn_ln_g"].T, "m_b": a["L1_ffn_ln_b"].T, "L1_ffn_b2": a["L1_ffn_b2"],
        "stack_qk": qk, "stack_v": v, "stack_scales": scales.reshape(DEPTH * D, 4),
        "stack_o": a["L0_ffn_Wo"].reshape(DEPTH, 8, D, D).transpose(0, 2, 1, 3).reshape(DEPTH * D, 8, D),
        "stack_w1": a["L0_ffn_W1"].reshape(DEPTH * D, 2 * F_IN),
        "stack_w2": a["L0_ffn_W2"][:, rows].reshape(DEPTH, 3, D, D).transpose(0, 2, 1, 3).reshape(DEPTH * D, 3, D),
        "stack_b1": hid.transpose(0, 2, 1).reshape(DEPTH * D, 6),
        "stack_vecs": np.stack([a["L0_ffn_ln_g"], a["L0_ffn_ln_b"], a["L0_ffn_b2"]], 2).reshape(DEPTH * D, 3),
    }


def kernel(**inputs):
    import concourse.bacc as _bacc
    from concourse.bass_utils import run_bass_kernel_spmd as _run

    nc = _bacc.Bacc("TRN2", target_bir_lowering=False, num_devices=1)
    arrays = {f"in_{n}": np.ascontiguousarray(v) for n, v in
              laid_out({k: np.asarray(v) for k, v in inputs.items()}).items()}
    ins = {n[3:]: nc.dram_tensor(n, v.shape, mybir.dt.from_np(v.dtype), kind="ExternalInput").ap()
           for n, v in arrays.items()}
    out = nc.dram_tensor("out_x", (D, N), F32, kind="ExternalOutput").ap()
    hybrid_program(nc, ins, out)
    r = _run(nc, [arrays], core_ids=[0])
    return np.ascontiguousarray(r.results[0]["out_x"].T).reshape(B, T, D)
```
